# Optimizing a Trainium2 kernel written in Bass

```python
import numpy as np
import jax
import jax.numpy as jnp

def _softmax(x, axis=-1):
    return jax.nn.softmax(x, axis=axis)

def _gelu(x):
    return jax.nn.gelu(x, approximate=True)

def _silu(x):
    return jax.nn.silu(x)

def _sigmoid(x):
    return jax.nn.sigmoid(x)

def _layernorm(x, axis=-1, eps=1e-05):
    m = jnp.mean(x, axis=axis, keepdims=True)
    v = jnp.var(x, axis=axis, keepdims=True)
    return (x - m) / jnp.sqrt(v + eps)

def _scatter_add(tgt, idx, src, axis=0):
    return tgt.at[idx].add(src)

def _segment_sum(src, seg, n):
    return jax.ops.segment_sum(src, seg, n)
kernel_name = 'mk_recurrent_d1_jaxref_r8_3ca12a'

def setup_inputs(seed: int=0):
    np.random.seed(seed)
    _w = jnp.asarray

    def _L0_attn_setup():
        import jax, jax.numpy as jnp
        import numpy as np
        D_MODEL, EXPAND, D_STATE, D_CONV, HEADDIM = (128, 2, 64, 4, 64)
        D_INNER = EXPAND * D_MODEL
        NHEADS = D_INNER // HEADDIM
        CONV_DIM = D_INNER + 2 * D_STATE
        D_IN_PROJ = 2 * D_INNER + 2 * D_STATE + NHEADS
        EPS = 1e-05

        def _layernorm(x, w, b):
            mu = jnp.mean(x, axis=-1, keepdims=True)
            var = jnp.mean(jnp.square(x - mu), axis=-1, keepdims=True)
            return (x - mu) * jax.lax.rsqrt(var + EPS) * w + b

        def _mamba2(x, in_proj_w, conv_w, conv_b, dt_bias, A_log, D, norm_w, out_proj_w):
            Bt, L, _ = x.shape
            zxbcdt = x @ in_proj_w.T
            z = zxbcdt[..., :D_INNER]
            xBC = zxbcdt[..., D_INNER:D_INNER + CONV_DIM]
            dt = jax.nn.softplus(zxbcdt[..., D_INNER + CONV_DIM:] + dt_bias)
            xp = jnp.pad(xBC, ((0, 0), (D_CONV - 1, 0), (0, 0)))
            conv = conv_b
            for k in range(D_CONV):
                conv = conv + xp[:, k:k + L, :] * conv_w[:, k]
            xBC = jax.nn.silu(conv)
            xs = xBC[..., :D_INNER].reshape(Bt, L, NHEADS, HEADDIM)
            Bm = xBC[..., D_INNER:D_INNER + D_STATE]
            Cm = xBC[..., D_INNER + D_STATE:]
            A = -jnp.exp(A_log)

            def step(h, inp):
                x_t, dt_t, B_t, C_t = inp
                dA = jnp.exp(dt_t * A)
                h = h * dA[:, :, None, None] + (dt_t[:, :, None] * x_t)[..., None] * B_t[:, None, None, :]
                y = jnp.einsum('bhpn,bn->bhp', h, C_t)
                return (h, y)
            h0 = jnp.zeros((Bt, NHEADS, HEADDIM, D_STATE), x.dtype)
            xsT = jnp.moveaxis(xs, 1, 0)
            dtT = jnp.moveaxis(dt, 1, 0)
            BT = jnp.moveaxis(Bm, 1, 0)
            CT = jnp.moveaxis(Cm, 1, 0)
            _, ys = jax.lax.scan(step, h0, (xsT, dtT, BT, CT))
            y = jnp.moveaxis(ys, 0, 1) + xs * D[None, None, :, None]
            y = y.reshape(Bt, L, D_INNER)
            y = y * jax.nn.silu(z)
            y = y * jax.lax.rsqrt(jnp.mean(jnp.square(y), axis=-1, keepdims=True) + EPS) * norm_w
            return y @ out_proj_w.T
        key = jax.random.key(seed)
        ks = jax.random.split(key, 16)
        s = 0.02
        inp = {'x': jax.random.normal(ks[0], (2, 256, D_MODEL), jnp.float32), 'ln1_w': jnp.ones((D_MODEL,), jnp.float32), 'ln1_b': jnp.zeros((D_MODEL,), jnp.float32), 'in_proj_w': jax.random.normal(ks[1], (D_IN_PROJ, D_MODEL), jnp.float32) * s, 'conv_w': jax.random.normal(ks[2], (CONV_DIM, D_CONV), jnp.float32) * 0.3, 'conv_b': jnp.zeros((CONV_DIM,), jnp.float32), 'dt_bias': jnp.log(jnp.expm1(jnp.exp(jax.random.uniform(ks[3], (NHEADS,), jnp.float32, jnp.log(0.001), jnp.log(0.1))))), 'A_log': jnp.log(jax.random.uniform(ks[4], (NHEADS,), jnp.float32, 1.0, 16.0)), 'D': jnp.ones((NHEADS,), jnp.float32), 'norm_w': jnp.ones((D_INNER,), jnp.float32), 'out_proj_w': jax.random.normal(ks[5], (D_MODEL, D_INNER), jnp.float32) * s, 'ln2_w': jnp.ones((D_MODEL,), jnp.float32), 'ln2_b': jnp.zeros((D_MODEL,), jnp.float32), 'mlp_w1': jax.random.normal(ks[6], (4 * D_MODEL, D_MODEL), jnp.float32) * s, 'mlp_b1': jnp.zeros((4 * D_MODEL,), jnp.float32), 'mlp_w2': jax.random.normal(ks[7], (D_MODEL, 4 * D_MODEL), jnp.float32) * s, 'mlp_b2': jnp.zeros((D_MODEL,), jnp.float32)}
        return inp
    _L0_attn_in = _L0_attn_setup()

    def _L0_ffn_setup():
        import jax, jax.numpy as jnp
        import numpy as np
        DIM = 128
        HEADS = 16
        HD = DIM // HEADS
        M = 32
        E = 4
        K = 2
        HID = 256
        MID = 256
        LB = 0.01
        EPS = 1.1920929e-07

        def _rms(x, w):
            return x * jax.lax.rsqrt(jnp.mean(x * x, axis=-1, keepdims=True) + EPS) * w

        def _gelu(x):
            return jax.nn.gelu(x, approximate=False)
        key = jax.random.key(seed)
        ks = jax.random.split(key, 20)
        d = DIM
        w = lambda k, s: jax.random.normal(k, s, jnp.float32) * 0.02
        return {'x': jax.random.normal(ks[0], (4, 128, d), jnp.float32), 'n1_w': jnp.ones((d,), jnp.float32), 'n2_w': jnp.ones((d,), jnp.float32), 'wq': w(ks[1], (d, d)), 'wk': w(ks[2], (d, d)), 'wv': w(ks[3], (d, d)), 'wo': w(ks[4], (d, d)), 'qn_w': jnp.ones((HD,), jnp.float32), 'kn_w': jnp.ones((HD,), jnp.float32), 'gate_w': w(ks[5], (E, d)), 'e0_up': w(ks[6], (HID, d)), 'e0_down': w(ks[7], (d, HID)), 'e1_w1': w(ks[8], (HID, d)), 'e1_w2': w(ks[9], (HID, d)), 'e1_down': w(ks[10], (d, HID)), 'e2_l1': w(ks[11], (MID, d)), 'e2_l2': w(ks[12], (HID, MID)), 'e2_l3': w(ks[13], (MID, HID)), 'e2_l4': w(ks[14], (d, MID)), 'e3_down': w(ks[15], (d, d)), 'e3_up': w(ks[16], (HID, d)), 'e3_out': w(ks[17], (d, HID))}
    _L0_ffn_in = _L0_ffn_setup()
    _d = {'L0_attn_x': _L0_attn_in['x'], 'L0_attn_ln1_w': _L0_attn_in['ln1_w'], 'L0_attn_ln1_b': _L0_attn_in['ln1_b'], 'L0_attn_in_proj_w': _L0_attn_in['in_proj_w'], 'L0_attn_conv_w': _L0_attn_in['conv_w'], 'L0_attn_conv_b': _L0_attn_in['conv_b'], 'L0_attn_dt_bias': _L0_attn_in['dt_bias'], 'L0_attn_A_log': _L0_attn_in['A_log'], 'L0_attn_D': _L0_attn_in['D'], 'L0_attn_norm_w': _L0_attn_in['norm_w'], 'L0_attn_out_proj_w': _L0_attn_in['out_proj_w'], 'L0_attn_ln2_w': _L0_attn_in['ln2_w'], 'L0_attn_ln2_b': _L0_attn_in['ln2_b'], 'L0_attn_mlp_w1': _L0_attn_in['mlp_w1'], 'L0_attn_mlp_b1': _L0_attn_in['mlp_b1'], 'L0_attn_mlp_w2': _L0_attn_in['mlp_w2'], 'L0_attn_mlp_b2': _L0_attn_in['mlp_b2'], 'L0_ffn_n1_w': _L0_ffn_in['n1_w'], 'L0_ffn_n2_w': _L0_ffn_in['n2_w'], 'L0_ffn_wq': _L0_ffn_in['wq'], 'L0_ffn_wk': _L0_ffn_in['wk'], 'L0_ffn_wv': _L0_ffn_in['wv'], 'L0_ffn_wo': _L0_ffn_in['wo'], 'L0_ffn_qn_w': _L0_ffn_in['qn_w'], 'L0_ffn_kn_w': _L0_ffn_in['kn_w'], 'L0_ffn_gate_w': _L0_ffn_in['gate_w'], 'L0_ffn_e0_up': _L0_ffn_in['e0_up'], 'L0_ffn_e0_down': _L0_ffn_in['e0_down'], 'L0_ffn_e1_w1': _L0_ffn_in['e1_w1'], 'L0_ffn_e1_w2': _L0_ffn_in['e1_w2'], 'L0_ffn_e1_down': _L0_ffn_in['e1_down'], 'L0_ffn_e2_l1': _L0_ffn_in['e2_l1'], 'L0_ffn_e2_l2': _L0_ffn_in['e2_l2'], 'L0_ffn_e2_l3': _L0_ffn_in['e2_l3'], 'L0_ffn_e2_l4': _L0_ffn_in['e2_l4'], 'L0_ffn_e3_down': _L0_ffn_in['e3_down'], 'L0_ffn_e3_up': _L0_ffn_in['e3_up'], 'L0_ffn_e3_out': _L0_ffn_in['e3_out']}
    _x0 = _d['L0_attn_x']
    _d['L0_attn_x'] = jax.random.normal(jax.random.fold_in(jax.random.key(seed), 1), (8, 512, 128), dtype=_x0.dtype)
    del _x0
    return _d

def reference(L0_attn_x, L0_attn_ln1_w, L0_attn_ln1_b, L0_attn_in_proj_w, L0_attn_conv_w, L0_attn_conv_b, L0_attn_dt_bias, L0_attn_A_log, L0_attn_D, L0_attn_norm_w, L0_attn_out_proj_w, L0_attn_ln2_w, L0_attn_ln2_b, L0_attn_mlp_w1, L0_attn_mlp_b1, L0_attn_mlp_w2, L0_attn_mlp_b2, L0_ffn_n1_w, L0_ffn_n2_w, L0_ffn_wq, L0_ffn_wk, L0_ffn_wv, L0_ffn_wo, L0_ffn_qn_w, L0_ffn_kn_w, L0_ffn_gate_w, L0_ffn_e0_up, L0_ffn_e0_down, L0_ffn_e1_w1, L0_ffn_e1_w2, L0_ffn_e1_down, L0_ffn_e2_l1, L0_ffn_e2_l2, L0_ffn_e2_l3, L0_ffn_e2_l4, L0_ffn_e3_down, L0_ffn_e3_up, L0_ffn_e3_out):

    def _L0_attn_ref(x, ln1_w, ln1_b, in_proj_w, conv_w, conv_b, dt_bias, A_log, D, norm_w, out_proj_w, ln2_w, ln2_b, mlp_w1, mlp_b1, mlp_w2, mlp_b2):
        import jax, jax.numpy as jnp
        import numpy as np
        D_MODEL, EXPAND, D_STATE, D_CONV, HEADDIM = (128, 2, 64, 4, 64)
        D_INNER = EXPAND * D_MODEL
        NHEADS = D_INNER // HEADDIM
        CONV_DIM = D_INNER + 2 * D_STATE
        D_IN_PROJ = 2 * D_INNER + 2 * D_STATE + NHEADS
        EPS = 1e-05

        def _layernorm(x, w, b):
            mu = jnp.mean(x, axis=-1, keepdims=True)
            var = jnp.mean(jnp.square(x - mu), axis=-1, keepdims=True)
            return (x - mu) * jax.lax.rsqrt(var + EPS) * w + b

        def _mamba2(x, in_proj_w, conv_w, conv_b, dt_bias, A_log, D, norm_w, out_proj_w):
            Bt, L, _ = x.shape
            zxbcdt = x @ in_proj_w.T
            z = zxbcdt[..., :D_INNER]
            xBC = zxbcdt[..., D_INNER:D_INNER + CONV_DIM]
            dt = jax.nn.softplus(zxbcdt[..., D_INNER + CONV_DIM:] + dt_bias)
            xp = jnp.pad(xBC, ((0, 0), (D_CONV - 1, 0), (0, 0)))
            conv = conv_b
            for k in range(D_CONV):
                conv = conv + xp[:, k:k + L, :] * conv_w[:, k]
            xBC = jax.nn.silu(conv)
            xs = xBC[..., :D_INNER].reshape(Bt, L, NHEADS, HEADDIM)
            Bm = xBC[..., D_INNER:D_INNER + D_STATE]
            Cm = xBC[..., D_INNER + D_STATE:]
            A = -jnp.exp(A_log)

            def step(h, inp):
                x_t, dt_t, B_t, C_t = inp
                dA = jnp.exp(dt_t * A)
                h = h * dA[:, :, None, None] + (dt_t[:, :, None] * x_t)[..., None] * B_t[:, None, None, :]
                y = jnp.einsum('bhpn,bn->bhp', h, C_t)
                return (h, y)
            h0 = jnp.zeros((Bt, NHEADS, HEADDIM, D_STATE), x.dtype)
            xsT = jnp.moveaxis(xs, 1, 0)
            dtT = jnp.moveaxis(dt, 1, 0)
            BT = jnp.moveaxis(Bm, 1, 0)
            CT = jnp.moveaxis(Cm, 1, 0)
            _, ys = jax.lax.scan(step, h0, (xsT, dtT, BT, CT))
            y = jnp.moveaxis(ys, 0, 1) + xs * D[None, None, :, None]
            y = y.reshape(Bt, L, D_INNER)
            y = y * jax.nn.silu(z)
            y = y * jax.lax.rsqrt(jnp.mean(jnp.square(y), axis=-1, keepdims=True) + EPS) * norm_w
            return y @ out_proj_w.T
        res = x
        h = _layernorm(x, ln1_w, ln1_b)
        h = _mamba2(h, in_proj_w, conv_w, conv_b, dt_bias, A_log, D, norm_w, out_proj_w)
        x = res + h
        res = x
        h = _layernorm(x, ln2_w, ln2_b)
        h = jax.nn.gelu(h @ mlp_w1.T + mlp_b1, approximate=False) @ mlp_w2.T + mlp_b2
        return res + h

    def _L0_ffn_ref(x, n1_w, n2_w, wq, wk, wv, wo, qn_w, kn_w, gate_w, e0_up, e0_down, e1_w1, e1_w2, e1_down, e2_l1, e2_l2, e2_l3, e2_l4, e3_down, e3_up, e3_out):
        import jax, jax.numpy as jnp
        import numpy as np
        DIM = 128
        HEADS = 16
        HD = DIM // HEADS
        M = 32
        E = 4
        K = 2
        HID = 256
        MID = 256
        LB = 0.01
        EPS = 1.1920929e-07

        def _rms(x, w):
            return x * jax.lax.rsqrt(jnp.mean(x * x, axis=-1, keepdims=True) + EPS) * w

        def _gelu(x):
            return jax.nn.gelu(x, approximate=False)
        B, T, C = x.shape
        h = _rms(x, n1_w)
        heads = lambda w_: (h @ w_.T).reshape(B, T, HEADS, HD).transpose(0, 2, 1, 3)
        q = _rms(heads(wq), qn_w)
        k = _rms(heads(wk), kn_w)
        v = heads(wv)
        scores = jnp.einsum('bhqd,bhkd->bhqk', q, k) * HD ** (-0.5)
        causal = jnp.tril(jnp.ones((T, T), bool))
        scores = jnp.where(causal[None, None], scores, -jnp.inf)
        attn = jax.nn.softmax(scores, axis=-1)
        ao = jnp.einsum('bhqk,bhkd->bhqd', attn, v).transpose(0, 2, 1, 3).reshape(B, T, C) @ wo.T
        ao = ao.at[:, :, :M].set(0.0)
        x = x + ao
        xf = _rms(x, n2_w).reshape(-1, C)
        N = xf.shape[0]
        logits = jnp.nan_to_num(xf @ gate_w.T)
        probs = jax.nn.softmax(logits, axis=-1)
        topv, topi = jax.lax.top_k(probs, K)
        topv = topv / (topv.sum(-1, keepdims=True) + 1e-08)
        wts = jnp.zeros((N, E), x.dtype).at[jnp.arange(N)[:, None], topi].add(topv)
        o0 = _gelu(xf @ e0_up.T) @ e0_down.T
        o1 = jax.nn.silu(xf @ e1_w1.T) * (xf @ e1_w2.T) @ e1_down.T
        o2 = _gelu(_gelu(_gelu(xf @ e2_l1.T) @ e2_l2.T) @ e2_l3.T) @ e2_l4.T
        o3 = _gelu(_gelu(xf @ e3_down.T) @ e3_up.T) @ e3_out.T
        moe = wts[:, 0:1] * o0 + wts[:, 1:2] * o1 + wts[:, 2:3] * o2 + wts[:, 3:4] * o3
        moe = moe.reshape(B, T, C).at[:, :, :M].set(0.0)
        return x + moe
    x = L0_attn_x
    xn = _layernorm(x, axis=-1)
    s = _L0_attn_ref(xn, L0_attn_ln1_w, L0_attn_ln1_b, L0_attn_in_proj_w, L0_attn_conv_w, L0_attn_conv_b, L0_attn_dt_bias, L0_attn_A_log, L0_attn_D, L0_attn_norm_w, L0_attn_out_proj_w, L0_attn_ln2_w, L0_attn_ln2_b, L0_attn_mlp_w1, L0_attn_mlp_b1, L0_attn_mlp_w2, L0_attn_mlp_b2)
    g = _silu(_L0_ffn_ref(xn, L0_ffn_n1_w, L0_ffn_n2_w, L0_ffn_wq, L0_ffn_wk, L0_ffn_wv, L0_ffn_wo, L0_ffn_qn_w, L0_ffn_kn_w, L0_ffn_gate_w, L0_ffn_e0_up, L0_ffn_e0_down, L0_ffn_e1_w1, L0_ffn_e1_w2, L0_ffn_e1_down, L0_ffn_e2_l1, L0_ffn_e2_l2, L0_ffn_e2_l3, L0_ffn_e2_l4, L0_ffn_e3_down, L0_ffn_e3_up, L0_ffn_e3_out))
    x = x + s * g
    return x

_drawn_inputs = setup_inputs


def setup_inputs(seed=0):
    import zlib

    import numpy as np

    out = dict(_drawn_inputs(seed))
    spreads = {'L0_attn_ln1_w': (1.0, 0.6),
     'L0_attn_ln1_b': (0.0, 0.655),
     'L0_attn_conv_b': (0.0, 0.1),
     'L0_attn_D': (1.0, 0.6),
     'L0_attn_norm_w': (1.0, 0.6),
     'L0_attn_ln2_w': (1.0, 0.6),
     'L0_attn_ln2_b': (0.0, 0.8),
     'L0_attn_mlp_b1': (0.0, 0.8),
     'L0_attn_mlp_b2': (0.0, 0.1),
     'L0_ffn_n1_w': (1.0, 0.6),
     'L0_ffn_n2_w': (1.0, 0.6),
     'L0_ffn_qn_w': (1.0, 0.6),
     'L0_ffn_kn_w': (1.0, 0.6)}
    factors = {'L0_attn_dt_bias': 8.0,
     'L0_attn_A_log': 8.0,
     'L0_attn_mlp_w1': 3.041,
     'L0_attn_mlp_w2': 2.752,
     'L0_ffn_wq': 8.0,
     'L0_ffn_wk': 8.0,
     'L0_ffn_wv': 8.0,
     'L0_ffn_wo': 8.0,
     'L0_ffn_gate_w': 8.0,
     'L0_ffn_e0_up': 8.0,
     'L0_ffn_e0_down': 8.0,
     'L0_ffn_e1_w1': 8.0,
     'L0_ffn_e1_w2': 8.0,
     'L0_ffn_e1_down': 8.0,
     'L0_ffn_e2_l1': 8.0,
     'L0_ffn_e2_l2': 8.0,
     'L0_ffn_e2_l3': 8.0,
     'L0_ffn_e2_l4': 8.0,
     'L0_ffn_e3_down': 8.0,
     'L0_ffn_e3_up': 8.0,
     'L0_ffn_e3_out': 8.0}
    for name, (base, spread) in spreads.items():
        noise = np.random.default_rng([zlib.crc32(name.encode()), seed]).standard_normal(out[name].shape)
        drawn = base * np.exp(spread * noise) if base else spread * noise
        out[name] = jnp.asarray(drawn.astype(out[name].dtype))
    for name, factor in factors.items():
        out[name] = (out[name] * factor).astype(out[name].dtype)
    return out
```

```python
from contextlib import ExitStack

import concourse.bass as bass
from concourse import mybir

F32 = mybir.dt.float32
F32R = mybir.dt.float32r
BF16 = mybir.dt.bfloat16
ALU = mybir.AluOpType
ACT = mybir.ActivationFunctionType
AX = mybir.AxisListType

P = 128
B, L, D = 8, 512, 128
T = L // P
NH, HP, NS = 4, 64, 64
DI = NH * HP
CONV = DI + 2 * NS
TAPS = 4
AH, HD = 16, 8
G = 4
E = 4
MASKED = 32
OC = D - MASKED
EPS = 1e-5
EPS_RMS = 1.1920929e-07
FMAX = 3.4028234663852886e38
NEG = -1e30
UNITS = 8

W_COLS = {}
_at = 0
for _name, _n in (("qkv", 3 * D), ("x", CONV), ("zdt", DI + NH), ("wo", OC), ("op", 2 * D),
                  ("gate", E), ("e0u", 256), ("e3a", 128), ("e2a", 256), ("w1", 512),
                  ("e3b", 256), ("e2b", 512), ("e2c", 512), ("e1a", 256), ("e1b", 256),
                  ("w2", 512), ("e0d", 2 * OC), ("e1d", 2 * OC), ("e2d", 2 * OC), ("e3d", 2 * OC)):
    W_COLS[_name] = (_at, _at + _n)
    _at += _n
W_TOTAL = _at
W_HEAD = W_COLS["zdt"][1]

V_LN1W, V_LN1B, V_N1W, V_LN2W, V_LN2B, V_N2W = range(6)
V_B1, V_NORM, V_CONVB, V_CONVW, V_DCH = 6, 10, 12, 15, 27
V_TOTAL = 29
R_DTB, R_ALOG, R_QN, R_KN, R_B2 = 0, 4, 8, 16, 24
R_TOTAL = 24 + D


def build(nc, x, weights, vectors, rows, consts, out):
    with ExitStack() as ctx:
        def sb(name, shape, dt=F32):
            return ctx.enter_context(nc.sbuf_tensor("sb_" + name, shape, dt))

        def ps(name, shape, dt=F32):
            return ctx.enter_context(nc.psum_tensor(name, shape, dt))

        per, lead, made = {}, {}, []

        def signal(name, per_round, ahead=0):
            sem = ctx.enter_context(nc.semaphore(name))
            per[sem.name], lead[sem.name] = per_round, ahead
            made.append(sem)
            return sem

        def at(sem, r, k):
            return (r + 2 + lead[sem.name]) * per[sem.name] + k

        W = sb("W", [P, W_TOTAL])
        vec = sb("vec", [P, V_TOTAL])
        row = sb("row", [P, R_TOTAL])
        cst = sb("cst", [P, 5 * P + 16])
        ident = cst[:, 0:P]
        upto = cst[:, P:2 * P]
        after = cst[:, 2 * P:3 * P]
        ones = cst[:, 3 * P:4 * P]
        future = cst[:, 4 * P:5 * P]
        before = cst[:, 5 * P:5 * P + 16].rearrange("p (e f) -> p e f", e=E)
        identb = sb("identb", [P, P], BF16)
        maskb = sb("maskb", [P, P], BF16)
        minus_half = sb("minus_half", [P, 8])
        wqk = sb("wqk", [P, 2, AH, HD])
        neg_a = sb("neg_a", [P, NH])
        diag_d = sb("diag_d", [P, 2, P])

        def w(name):
            a, b = W_COLS[name]
            return W[:, a:b]

        def w2(name, n):
            return w(name).rearrange("p (h n) -> p h n", n=n)

        xin = sb("xin", [P, T, D])
        xres = sb("xres", [P, T, D])
        xn = sb("xn", [P, T, D])
        xa = sb("xa", [P, T, D])
        xb = sb("xb", [P, T, D])
        xaT = sb("xaT", [P, L])
        xbT = sb("xbT", [P, L])
        st6 = sb("st6", [P, T, 6])
        mv = sb("mv", [P, T, 2])
        lnv = sb("lnv", [P, 8, T])
        qk = sb("qk", [P, T, 2, AH, HD])
        sq = sb("sq", [P, T, 2, AH, HD])
        rqk = sb("rqk", [P, 3, T * 2 * AH])
        tokqk = sb("tokqk", [P, T, 2, AH, 32])
        qT = sb("qT", [P, G, L], F32R)
        kT = sb("kT", [P, G, L], F32R)
        va = sb("va", [P, T, AH, 32])
        mx = sb("mx", [P, T, G, 4])
        mhl = sb("mhl", [P, G, T, 4, 2])
        mT = sb("mT", [8, 2, L], F32R)
        pr = sb("pr", [P, 4, 2, L])
        oT = sb("oT", [P, 2, L])
        rden = sb("rden", [P, T, 4])
        ao = sb("ao", [P, T, D])
        aoT = sb("aoT", [P, L])
        xc = sb("xc", [P, 3, L + 3])
        cv = sb("cv", [P, 3, L])
        cm = sb("cm", [P, L])
        xact = sb("xact", [P, 3, L])
        cT = sb("cT", [NS, L])
        zraw = sb("zraw", [P, T, DI + NH])
        zs = zraw[:, :, 0:DI]
        sp = sb("sp", [P, 10, T, NH])
        dt = sb("dt", [P, T, NH])
        dta = sb("dta", [P, T, NH])
        dec = sb("dec", [P, 3, T, NH])
        rs = sb("rs", [P, 2, NH, P])
        es = sb("es", [P, 2, NH, P])
        gm = sb("gm", [P, 2, P])
        wm = sb("wm", [P, 2, NH, P])
        xdt = sb("xdt", [P, 2, DI])
        xw = sb("xw", [P, 2, DI])
        btok = sb("btok", [P, 2, NS])
        hst = sb("hst", [NS, DI])
        hdec = sb("hdec", [NS, DI])
        yc = sb("yc", [P, 2, DI])
        yz = sb("yz", [P, 2, DI])
        junk = sb("junk", [P, 2, DI])
        yss = sb("yss", [P, T])
        ry = sb("ry", [P, 3, T])
        yT = sb("yT", [P, 2, L])
        x1 = sb("x1", [P, T, D])
        x1n = sb("x1n", [P, T, D])
        x1T = sb("x1T", [P, L])
        st2 = sb("st2", [P, T, 6])
        mv2 = sb("mv2", [P, T, 2])
        r2 = sb("r2", [P, 2, T])
        x2 = sb("x2", [P, T, D])
        x2ss = sb("x2ss", [P, T])
        r3 = sb("r3", [P, 3, T])
        xf = sb("xf", [P, T, D])
        xfT = sb("xfT", [P, L])
        gt = sb("gt", [P, 12, T, E])
        g1 = sb("g1", [P, 4, T])
        gq = sb("gq", [P, 2, T, E, E])
        wts = sb("wts", [P, T, E])
        share = pr[:].rearrange("p a h l -> p (a h) l")
        hm, h0, h2c = share[:, 0:4], share[:, 4:6], share[:, 6:8]
        h2a = rs[:].rearrange("p k h t -> p k (h t)")
        h2b = es[:].rearrange("p k h t -> p k (h t)")
        h1a = wm[:].rearrange("p k h t -> p k (h t)")
        h1 = sb("h1", [P, 2, L])
        h3a = sb("h3a", [P, L])
        h3b = sb("h3b", [P, 2, L])
        gs = sb("gs", [P, T, D])

        S = [ps(f"S{i}", [P, 2, L]) for i in range(2)]
        R = [ps(f"R{i}", [P, L]) for i in range(4)]

        def bank(i):
            return S[i // 2][:, i % 2, :]

        c_loaded = signal("c_loaded", 0)
        wh_loaded = signal("wh_loaded", 0)
        wt_loaded = signal("wt_loaded", 0)
        x_loaded = signal("x_loaded", 16, 1)
        xres_loaded = signal("xres_loaded", 16)
        c_moved = signal("c_moved", 16)
        m_moved = [signal(f"m_moved{g}", 4 * 16) for g in range(G)]
        out_stored = signal("out_stored", 16)

        pool_set = signal("pool_set", 0)
        dve_set = signal("dve_set", 0)
        act_set = signal("act_set", 0)

        pool_passed = signal("pool_passed", 0)
        dve_passed = signal("dve_passed", 0)

        made.clear()
        qkv_ps = signal("qkv_ps", T)
        xbc_ps = signal("xbc_ps", 3)
        z_ps = signal("z_ps", T)
        op_ps = signal("op_ps", 1)
        ot_ps = signal("ot_ps", G - 1)
        ot3_ps = signal("ot3_ps", 1)
        aoT_ps = signal("aoT_ps", 1)
        wo_ps = signal("wo_ps", 1)
        xfT_ps = signal("xfT_ps", 1)
        x1T_ps = signal("x1T_ps", 1)
        gate_ps = signal("gate_ps", 1)
        up_ps = signal("up_ps", 19)
        qkT_ps = signal("qkT_ps", 2 * G)
        s_ps = signal("s_ps", G * UNITS)
        mT_ps = signal("mT_ps", G)
        e_ps = signal("e_ps", G * UNITS)
        pv_ps = signal("pv_ps", G * UNITS)
        cum_ps = signal("cum_ps", 1)
        seg_ps = signal("seg_ps", T)
        xt_ps = signal("xt_ps", T)
        y_ps = signal("y_ps", T)
        hn_ps = signal("hn_ps", T - 1)
        yT_ps = signal("yT_ps", T)
        mlp_ps = signal("mlp_ps", 1)
        moe_ps = signal("moe_ps", T)
        xaT_ps = signal("xaT_ps", 1, 1)
        xbT_ps = signal("xbT_ps", 1, 1)

        pe_sems = made[:]
        made.clear()
        qkv_sb = signal("qkv_sb", T)
        sq_sb = signal("sq_sb", 1)
        xc_sb = signal("xc_sb", 3)
        rqk_sb = signal("rqk_sb", 2)
        z_sb = signal("z_sb", T)
        aoT_sb = signal("aoT_sb", 1)
        x2ss_sb = signal("x2ss_sb", 1)
        xfT_sb = signal("xfT_sb", 1)
        x1T_sb = signal("x1T_sb", 1)
        gexp_sb = signal("gexp_sb", 1)
        spe_sb = signal("spe_sb", 1)
        qT_sb = signal("qT_sb", G)
        mT_sb = signal("mT_sb", G)
        act_up = signal("act_up", 17)
        conv_sb = signal("conv_sb", 1)
        zs_sb = signal("zs_sb", 1)
        dec_sb = signal("dec_sb", 1)
        seg_sb = signal("seg_sb", T)
        p_sb = signal("p_sb", G * UNITS)
        oT_sb = signal("oT_sb", G)
        yss_sb = signal("yss_sb", T)
        yT_sb = signal("yT_sb", T)
        xaT_sb = signal("xaT_sb", 1, 1)
        xbT_sb = signal("xbT_sb", 1, 1)
        gs_sb = signal("gs_sb", 1)

        act_sems = made[:]
        made.clear()
        ao_sb = signal("ao_sb", 2 * (G - 1))
        ao3_sb = signal("ao3_sb", 2)
        x1_sb = signal("x1_sb", T)
        ssqk_sb = signal("ssqk_sb", 2)
        ln2_sb = signal("ln2_sb", 2)
        x2_sb = signal("x2_sb", 2)
        nqk_sb = signal("nqk_sb", 3)
        lo_sb = signal("lo_sb", 1)
        xf_sb = signal("xf_sb", 1)
        x1n_sb = signal("x1n_sb", 1)
        gate_sb = signal("gate_sb", 6)
        wts_sb = signal("wts_sb", 13)
        spa_sb = signal("spa_sb", 2)
        dt_sb = signal("dt_sb", 15)
        kT_sb = signal("kT_sb", G)
        conv_dve = signal("conv_dve", 2 * TAPS)
        mx_sb = signal("mx_sb", G * UNITS)
        mhl_sb = signal("mhl_sb", 2 * G)
        h1_sb = signal("h1_sb", 2)
        sv_sb = signal("sv_sb", 1)
        moe_sb = signal("moe_sb", T * E)
        xn_sb = signal("xn_sb", 1)
        xdt_sb = signal("xdt_sb", T)
        gm_sb = signal("gm_sb", T)
        wm_sb = signal("wm_sb", T)
        yc_sb = signal("yc_sb", 2 * (T - 1))
        yz_sb = signal("yz_sb", T)
        h_sb = signal("h_sb", 1 + 2 * (T - 2))
        stat_sb = signal("stat_sb", 2, 1)
        xab_sb = signal("xab_sb", 1, 1)

        dve_sems = made[:]
        made.clear()
        ry_sb = signal("ry_sb", 2)
        r2_sb = signal("r2_sb", 2)
        r3_sb = signal("r3_sb", 2)
        x1b_sb = signal("x1b_sb", 1)
        dup_sb = signal("dup_sb", 1)
        conv_pool = signal("conv_pool", 2 * TAPS - 1)
        rs_sb = signal("rs_sb", T)
        pm_sb = signal("pm_sb", G * UNITS)
        xw_sb = signal("xw_sb", T - 1)
        rn_sb = signal("rn_sb", 8, 1)
        og_sb = signal("og_sb", 2)

        pool_sems = made[:]

        block = ctx.enter_context(nc.Block())

        def unit(u):
            return u // 2, u % 2

        @block.sync
        def _(sp_e):
            for sem in (x_loaded, xres_loaded, c_moved, *m_moved, out_stored):
                sp_e.sem_inc(sem, per[sem.name])
            sp_e.dma_start(xin[:], x[0].rearrange("(t p) c -> p t c", p=P)).then_inc(x_loaded, 16)
            sp_e.dma_start(cst[:], consts).then_inc(c_loaded, 16)
            sp_e.dma_start(vec[:], vectors).then_inc(c_loaded, 16)
            sp_e.dma_start(row[:], rows).then_inc(c_loaded, 16)
            sp_e.dma_start(W[:, 0:W_HEAD], weights[:, 0:W_HEAD]).then_inc(wh_loaded, 16)
            sp_e.dma_start(W[:, W_HEAD:W_TOTAL], weights[:, W_HEAD:W_TOTAL]).then_inc(wt_loaded, 16)
            sp_e.sem_inc(xres_loaded, 16)
            sp_e.sem_inc(out_stored, 16)

            def move_maxima(r, g):
                sp_e.wait_ge(mT_sb, at(mT_sb, r, g + 1))
                for j in range(4):
                    sp_e.dma_start(qT[32 * j + 24:32 * j + 26, g, :].bitcast(F32),
                                   mT[2 * j:2 * j + 2, g % 2, :].bitcast(F32))\
                        .then_inc(m_moved[g], 16)

            def rnd(r, tail, head, nxt):
                if tail:
                    sp_e.wait_ge(out_stored, at(out_stored, r, 0))
                    sp_e.dma_start(xres[:], x[r].rearrange("(t p) c -> p t c", p=P))\
                        .then_inc(xres_loaded, 16)
                if head:
                    move_maxima(r, 0)
                    move_maxima(r, 1)
                    sp_e.wait_ge(conv_sb, at(conv_sb, r, 1))
                    sp_e.wait_ge(y_ps, at(y_ps, r, 0))
                    sp_e.dma_start(cT[:], xact[NS:2 * NS, 2, :]).then_inc(c_moved, 16)
                    sp_e.wait_ge(xn_sb, at(xn_sb, r, 1))
                    sp_e.wait_ge(xab_sb, at(xab_sb, r, 0))
                    sp_e.dma_start(xin[:], x[nxt].rearrange("(t p) c -> p t c", p=P))\
                        .then_inc(x_loaded, 16)
                    move_maxima(r, 2)
                if tail:
                    sp_e.wait_ge(og_sb, at(og_sb, r, 2))
                    sp_e.dma_start(out[r].rearrange("(t p) c -> p t c", p=P), xres[:])\
                        .then_inc(out_stored, 16)
                if head:
                    move_maxima(r, 3)

            rnd(-1, False, True, 1)
            with sp_e.Fori(0, B - 2) as r:
                rnd(r, True, True, r + 2)
            rnd(B - 2, True, True, B - 1)
            rnd(B - 1, True, False, None)
            sp_e.wait_ge(out_stored, at(out_stored, B - 1, 16))

        @block.tensor
        def _(pe):
            def mm(o, lhsT, rhs, start=True, stop=True):
                return pe.matmul(o, lhsT, rhs, start=start, stop=stop, skip_group_check=True)

            def transposes(o, src):
                for t in range(T):
                    i = pe.transpose(o[:, t * P:(t + 1) * P], src(t), ident)
                return i

            def prep_a(r):
                pe.wait_ge(xab_sb, at(xab_sb, r, 1))
                pe.wait_ge(seg_sb, at(seg_sb, r, T))
                transposes(R[1], lambda t: xa[:, t, :]).then_inc(xaT_ps, 1)

            def prep_b(r):
                pe.wait_ge(xaT_sb, at(xaT_sb, r, 1))
                transposes(R[1], lambda t: xb[:, t, :]).then_inc(xbT_ps, 1)

            def max_scores(r, g, u):
                i, pair = unit(u)
                m = UNITS * g + u
                which = u % 2 if g < 2 else 0
                if m == 0 or m == 1:
                    pe.wait_ge(qT_sb, at(qT_sb, r, G))
                    pe.wait_ge(kT_sb, at(kT_sb, r, G))
                elif g < 2:
                    pe.wait_ge(mx_sb, at(mx_sb, r, m - 1))
                elif m == 2 * UNITS:
                    pe.wait_ge(mx_sb, at(mx_sb, r, m - 1))
                else:
                    pe.wait_ge(mx_sb, at(mx_sb, r, m))
                n = P * (i + 1)
                for h in range(2):
                    j = 32 * (2 * pair + h)
                    mm(S[which][:, h, 0:n], qT[j:j + 32, g, i * P:(i + 1) * P], kT[j:j + 32, g, 0:n],
                       True, False)
                for h in range(2):
                    o = mm(S[which][:, h, i * P:(i + 1) * P], identb[:], maskb[:], False, True)
                o.then_inc(s_ps, 1)

            def turn_maxima(r, g, o):
                pe.wait_ge(mhl_sb, at(mhl_sb, r, 2 * g + 2))
                if g >= 2:
                    pe.wait_ge(seg_sb, at(seg_sb, r, g))
                for t in range(T):
                    i = pe.transpose(o[0:8, t * P:(t + 1) * P],
                                     mhl[:, g, t].rearrange("p j x -> p (j x)"), ident)
                i.then_inc(mT_ps, 1)

            def exp_scores(r, g, u):
                i, pair = unit(u)
                e = UNITS * g + u
                which = 1 if g < 2 else u % 2
                if e == 0:
                    pe.wait_ge(mx_sb, at(mx_sb, r, 2 * UNITS))
                elif g < 2:
                    pe.wait_ge(p_sb, at(p_sb, r, e))
                elif e == 2 * UNITS:
                    pe.wait_ge(mx_sb, at(mx_sb, r, 4 * UNITS))
                elif e == 2 * UNITS + 1:
                    pe.wait_ge(p_sb, at(p_sb, r, e - 1))
                else:
                    pe.wait_ge(p_sb, at(p_sb, r, e - 1))
                if u == 0:
                    pe.wait_ge(m_moved[g], at(m_moved[g], r, 64))
                n = L - P * i
                for h in range(2):
                    j = 32 * (2 * pair + h)
                    o = mm(S[which][:, h, 0:n], kT[j:j + 32, g, i * P:(i + 1) * P],
                           qT[j:j + 32, g, i * P:L])
                o.then_inc(e_ps, 1)

            def weigh_values(r, g, u):
                i, pair = unit(u)
                e = UNITS * g + u
                pe.wait_ge(pm_sb, at(pm_sb, r, e + 1))
                pe.wait_ge(p_sb, at(p_sb, r, e + 1))
                if u == 0:
                    if g == 0:
                        pe.wait_ge(moe_sb, at(moe_sb, r, 3 * E))
                    else:
                        pe.wait_ge(oT_sb, at(oT_sb, r, g))
                n = L - P * i
                for h in range(2):
                    j = 2 * pair + h
                    o = mm(R[0][32 * j:32 * j + 32, i * P:L], va[:, i, 4 * g + j, :],
                           pr[:, e % 4, h, 0:n], i == 0, i == T - 1)
                o.then_inc(pv_ps, 1)

            def turn_values(r, g):
                pe.wait_ge(oT_sb, at(oT_sb, r, g + 1))
                pe.wait_ge(yz_sb, at(yz_sb, r, g + 1))
                for t in range(T):
                    i = pe.transpose(R[3][:, t * P:(t + 1) * P], oT[:, g % 2, t * P:(t + 1) * P], ident)
                i.then_inc(ot_ps, 1)

            def cumulate(r):
                pe.wait_ge(dt_sb, at(dt_sb, r, 15))
                pe.wait_ge(moe_sb, at(moe_sb, r, 4 * E))
                pe.wait_ge(mT_sb, at(mT_sb, r, 2))
                flat = dta[:].rearrange("p c h -> p (c h)")
                for n, lhs in enumerate((upto, after, ones)):
                    i = mm(R[1][:, 16 * n:16 * n + 16], lhs, flat)
                i.then_inc(cum_ps, 1)

            def segments(r, c):
                pe.wait_ge(rs_sb, at(rs_sb, r, c + 1))
                if c == 0:
                    pe.wait_ge(dec_sb, at(dec_sb, r, 1))
                elif c == 1:
                    pe.wait_ge(h_sb, at(h_sb, r, 1))
                else:
                    pe.wait_ge(h_sb, at(h_sb, r, 2 * c - 1))
                mm(R[1][:, :], after, rs[:, c % 2].rearrange("p h t -> p (h t)")).then_inc(seg_ps, 1)

            def scan_inputs(r, c):
                s = slice(c * P, (c + 1) * P)
                pe.wait_ge(conv_sb, at(conv_sb, r, 1))
                pe.wait_ge(c_moved, at(c_moved, r, 16))
                if c == 0:
                    pe.wait_ge(moe_sb, at(moe_sb, r, E))
                else:
                    pe.wait_ge(yT_sb, at(yT_sb, r, c))
                for n in range(3):
                    pe.transpose(R[2][:, n * P:(n + 1) * P], xact[:, n, s], ident)
                mm(R[2][:, 3 * P:4 * P], xact[0:NS, 2, s], cT[:, s]).then_inc(xt_ps, 1)

            def scan_outputs(r, c):
                s = slice(c * P, (c + 1) * P)
                pe.wait_ge(wm_sb, at(wm_sb, r, c + 1))
                pe.wait_ge(xdt_sb, at(xdt_sb, r, c + 1))
                if c == 0:
                    pe.wait_ge(moe_sb, at(moe_sb, r, 2 * E))
                else:
                    pe.wait_ge(h_sb, at(h_sb, r, 2 * c - 1))
                    pe.wait_ge(ao_sb, at(ao_sb, r, 2 * c))
                    mm(R[3][:, DI:2 * DI], cT[:, s], hst[:], True, False)
                for n in range(2):
                    mm(R[3][:, n * P:(n + 1) * P], xact[:, n, s], diag_d[:, n, :], c == 0 and n == 0, False)
                for h in range(NH):
                    i = mm(R[3][:, h * HP:(h + 1) * HP], wm[:, c % 2, h, :],
                           xdt[:, c % 2, h * HP:(h + 1) * HP], False, True)
                i.then_inc(y_ps, 1)

            def new_state(r, c):
                pe.wait_ge(xw_sb, at(xw_sb, r, c + 1))
                pe.wait_ge(gm_sb, at(gm_sb, r, c + 1))
                pe.wait_ge(seg_sb, at(seg_sb, r, c + 1))
                if c >= 1:
                    pe.wait_ge(mT_sb, at(mT_sb, r, c + 2))
                mm(R[1][0:NS, 0:DI], btok[:, c % 2, :], xw[:, c % 2, :]).then_inc(hn_ps, 1)

            def turn_y(r, c):
                pe.wait_ge(yz_sb, at(yz_sb, r, c + 1))
                pe.wait_ge(gm_sb, at(gm_sb, r, c + 1))
                for n in range(2):
                    i = pe.transpose(R[2][:, n * P:(n + 1) * P], yz[:, c % 2, n * P:(n + 1) * P], ident)
                i.then_inc(yT_ps, 1)

            def ring_free(r, k):
                if k == 0:
                    pe.wait_ge(xfT_sb, at(xfT_sb, r, 1))
                elif k == 1:
                    pe.wait_ge(x1T_sb, at(x1T_sb, r, 1))
                elif k == 2:
                    pe.wait_ge(gate_sb, at(gate_sb, r, 1))
                elif k == 3:
                    pe.wait_ge(x2_sb, at(x2_sb, r, 2))
                elif k - 4 <= 14:
                    pe.wait_ge(act_up, at(act_up, r, k - 3))
                elif k - 4 == 15:
                    pe.wait_ge(mT_sb, at(mT_sb, r, 1))
                elif k - 4 in (16, 17):
                    pe.wait_ge(act_up, at(act_up, r, k - 4))
                elif k - 4 in (18, 19):
                    pe.wait_ge(h1_sb, at(h1_sb, r, k - 21))
                elif k - 4 == 20:
                    pe.wait_ge(sv_sb, at(sv_sb, r, 1))
                else:
                    pe.wait_ge(mT_sb, at(mT_sb, r, 2))

            def up(r, k, name, n, src, ins=None):
                ring_free(r, k)
                if ins is not None:
                    pe.wait_ge(act_up, at(act_up, r, ins))
                if len(src) == 1:
                    lhs = [w(name)[:, n * P:(n + 1) * P]]
                else:
                    lhs = [w2(name, 256)[:, kk, n * P:(n + 1) * P] for kk in range(2)]
                for kk, (a, b) in enumerate(zip(lhs, src)):
                    i = mm(R[k % 4][:, :], a, b, kk == 0, kk == len(src) - 1)
                i.then_inc(up_ps, 1)

            def stage_b(r, tail, head):
                if tail:
                    pe.wait_ge(yT_sb, at(yT_sb, r, 0))
                    for t in range(T):
                        for n in range(2):
                            i = mm(R[2][:, t * P:(t + 1) * P], yT[:, n, t * P:(t + 1) * P],
                                   w2("op", D)[:, n, :], n == 0, n == 1)
                    i.then_inc(op_ps, 1)
                if head:
                    pe.wait_ge(xbT_sb, at(xbT_sb, r, 0))
                    pe.wait_ge(p_sb, at(p_sb, r, 0))
                    for t in range(T):
                        mm(bank(t)[:, 0:3 * D], xbT[:, t * P:(t + 1) * P], w("qkv")).then_inc(qkv_ps, 1)
                if tail:
                    pe.wait_ge(oT_sb, at(oT_sb, r, 0))
                    pe.wait_ge(yz_sb, at(yz_sb, r, 0))
                    for t in range(T):
                        i = pe.transpose(R[3][:, t * P:(t + 1) * P], oT[:, 1, t * P:(t + 1) * P], ident)
                    i.then_inc(ot3_ps, 1)
                if head:
                    for n in range(3):
                        pe.wait_ge(qkv_sb, at(qkv_sb, r, n + 1))
                        mm(bank(n), w("x")[:, n * P:(n + 1) * P], xaT[:]).then_inc(xbc_ps, 1)
                if tail:
                    pe.wait_ge(ao3_sb, at(ao3_sb, r, 2))
                    transposes(R[0], lambda t: ao[:, t, :]).then_inc(aoT_ps, 1)
                if head:
                    for t in (3, 0, 1, 2):
                        if t == 3:
                            pe.wait_ge(qkv_sb, at(qkv_sb, r, T))
                        else:
                            pe.wait_ge(xc_sb, at(xc_sb, r, t + 1))
                        mm(bank(t)[:, 0:DI + NH], xaT[:, t * P:(t + 1) * P], w("zdt")).then_inc(z_ps, 1)
                if tail:
                    pe.wait_ge(aoT_sb, at(aoT_sb, r, 1))
                    for t in range(T):
                        i = mm(R[3][:, t * OC:(t + 1) * OC], aoT[:, t * P:(t + 1) * P], w("wo"))
                    i.then_inc(wo_ps, 1)
                    pe.wait_ge(x1n_sb, at(x1n_sb, r, 1))
                    pe.wait_ge(xbT_sb, at(xbT_sb, r, 0))
                    transposes(R[1], lambda t: x1n[:, t, :]).then_inc(x1T_ps, 1)
                    pe.wait_ge(xf_sb, at(xf_sb, r, 1))
                    transposes(R[0], lambda t: xf[:, t, :]).then_inc(xfT_ps, 1)
                    pe.wait_ge(xfT_sb, at(xfT_sb, r, 1))
                    pe.wait_ge(x1_sb, at(x1_sb, r, T))
                    for t in range(T):
                        i = mm(R[2][:, t * E:(t + 1) * E], xfT[:, t * P:(t + 1) * P], w("gate"))
                    i.then_inc(gate_ps, 1)
                    up(r, 0, "e0u", 0, [xfT[:]])
                    up(r, 1, "e0u", 1, [xfT[:]])
                    up(r, 2, "e3a", 0, [xfT[:]])
                if head:
                    for n in range(2 * G):
                        if n == 0:
                            pe.wait_ge(lo_sb, at(lo_sb, r, 1))
                            pe.wait_ge(dup_sb, at(dup_sb, r, 1))
                        if n < T:
                            pe.wait_ge(z_sb, at(z_sb, r, (2, 3, 4, 1)[n]))
                        elif n % 2 == 0:
                            pe.wait_ge(qT_sb, at(qT_sb, r, (n - 4) // 2 + 1))
                        else:
                            pe.wait_ge(kT_sb, at(kT_sb, r, (n - 4) // 2 + 1))
                        transposes(bank(n % 4),
                                   lambda t: tokqk[:, t, n % 2, 4 * (n // 2):4 * (n // 2) + 4, :]
                                   .rearrange("p j x -> p (j x)")).then_inc(qkT_ps, 1)

                def m_unit(m):
                    if head:
                        max_scores(r, m // UNITS, m % UNITS)

                x_in = [xfT[:]]
                if tail:
                    up(r, 3, "e2a", 0, x_in)
                m_unit(0)
                if tail:
                    up(r, 4, "e2a", 1, x_in)
                m_unit(1)
                if tail:
                    up(r, 5, "w1", 0, [x1T[:]])
                m_unit(2)
                if tail:
                    up(r, 6, "w1", 1, [x1T[:]])
                m_unit(3)
                if tail:
                    up(r, 7, "e3b", 0, [h3a[:]], 3)
                m_unit(4)
                if tail:
                    up(r, 8, "e3b", 1, [h3a[:]])
                m_unit(5)
                if tail:
                    up(r, 9, "e2b", 0, [h2a[:, 0], h2a[:, 1]], 5)
                m_unit(6)
                if tail:
                    up(r, 10, "e2b", 1, [h2a[:, 0], h2a[:, 1]])
                m_unit(7)
                if tail:
                    up(r, 11, "w1", 2, [x1T[:]])
                m_unit(8)
                if tail:
                    up(r, 12, "w1", 3, [x1T[:]])
                m_unit(9)
                if tail:
                    up(r, 13, "e2c", 0, [h2b[:, 0], h2b[:, 1]], 11)
                m_unit(10)
                if tail:
                    up(r, 14, "e2c", 1, [h2b[:, 0], h2b[:, 1]])
                m_unit(11)
                if head:
                    ring_free(r, 15)
                    turn_maxima(r, 0, R[3])
                if tail:
                    up(r, 16, "e1a", 0, x_in)
                m_unit(12)
                if tail:
                    up(r, 17, "e1a", 1, x_in)
                m_unit(13)
                if tail:
                    up(r, 18, "e1b", 0, x_in)
                m_unit(14)
                if tail:
                    if head:
                        ring_free(r, 19)
                    else:
                        pe.wait_ge(act_up, at(act_up, r, 12))
                    mm(R[19 % 4][:, :], w("e1b")[:, P:2 * P], xfT[:]).then_inc(up_ps, 1)
                m_unit(15)
                if tail:
                    ring_free(r, 20)
                    pe.wait_ge(act_up, at(act_up, r, 13))
                    for t in range(T):
                        for n in range(4):
                            i = mm(R[0][:, t * P:(t + 1) * P], hm[:, n, t * P:(t + 1) * P],
                                   w("w2")[:, n * D:(n + 1) * D], n == 0, n == 3)
                    i.then_inc(mlp_ps, 1)
                if head:
                    ring_free(r, 21)
                    turn_maxima(r, 1, R[1])
                if tail:
                    for t in range(T):
                        if t == 3 and not head:
                            pe.wait_ge(act_up, at(act_up, r, 17))
                        else:
                            ring_free(r, 22 + t)
                        if t == 0:
                            pe.wait_ge(act_up, at(act_up, r, 17))
                            pe.wait_ge(h1_sb, at(h1_sb, r, 2))
                        for e, (h, name) in enumerate(((h0, "e0d"), (h1, "e1d"), (h2c, "e2d"), (h3b, "e3d"))):
                            for n in range(2):
                                i = mm(R[(22 + t) % 4][:, e * OC:(e + 1) * OC], h[:, n, t * P:(t + 1) * P],
                                       w2(name, OC)[:, n, :], n == 0, n == 1)
                        i.then_inc(moe_ps, 1)

            def stage_a(r):
                exp_scores(r, 0, 0)
                cumulate(r)
                for g in range(G):
                    for u in range(UNITS):
                        e = UNITS * g + u
                        if e > 0:
                            exp_scores(r, g, u)
                        if g < 2:
                            max_scores(r, g + 2, u)
                        if e > 0:
                            weigh_values(r, (e - 1) // UNITS, (e - 1) % UNITS)
                        if u == 0:
                            segments(r, g)
                            scan_inputs(r, g)
                        if u == 2:
                            if g in (1, 2):
                                turn_maxima(r, g + 1, R[1])
                            if g >= 1:
                                turn_values(r, g - 1)
                        if u == 3:
                            scan_outputs(r, g)
                        if u == 4 and g < T - 1:
                            new_state(r, g)
                        if u == 7:
                            turn_y(r, g)
                        if g == 3 and u == 4:
                            prep_a(r)
                        if g == 3 and u == 6:
                            prep_b(r)
                weigh_values(r, G - 1, UNITS - 1)

            for sem in pe_sems:
                pe.sem_inc(sem, per[sem.name])
            for sem in (op_ps, ot3_ps, aoT_ps, wo_ps, xfT_ps, x1T_ps, gate_ps, up_ps, mlp_ps, moe_ps):
                pe.sem_inc(sem, per[sem.name])
            pe.wait_ge(c_loaded, 48)
            pe.wait_ge(pool_set, 6)
            pe.wait_ge(dve_set, 7)
            pe.wait_ge(xab_sb, at(xab_sb, -2, 1))
            transposes(R[1], lambda t: xa[:, t, :]).then_inc(xaT_ps, 1)
            pe.wait_ge(xaT_sb, at(xaT_sb, -2, 1))
            transposes(R[1], lambda t: xb[:, t, :]).then_inc(xbT_ps, 1)
            pe.wait_ge(wh_loaded, 16)
            stage_b(-1, False, True)
            stage_a(-1)
            pe.wait_ge(wt_loaded, 16)
            with pe.Fori(0, B - 1) as r:
                stage_b(r, True, True)
                stage_a(r)
            stage_b(B - 1, True, False)

        @block.scalar
        def _(act):
            def evac_qkv(r):
                act.wait_ge(lo_sb, at(lo_sb, r, 0))
                act.wait_ge(pv_ps, at(pv_ps, r, 0))
                for t in range(T):
                    act.wait_ge(qkv_ps, at(qkv_ps, r, t + 1))
                    act.activation(qk[:, t].rearrange("p a h d -> p (a h d)"), bank(t)[:, 0:2 * D], ACT.Copy)
                    act.activation(va[:, t, :, 0:HD],
                                   bank(t)[:, 2 * D:3 * D].rearrange("p (h d) -> p h d", h=AH),
                                   ACT.Copy).then_inc(qkv_sb, 1)

            def evac_maxima(r, g, o):
                act.wait_ge(mT_ps, at(mT_ps, r, g + 1))
                if g < 2:
                    act.wait_ge(m_moved[g + 2], at(m_moved[g + 2], r, 0))
                else:
                    act.wait_ge(m_moved[g - 2], at(m_moved[g - 2], r, 64))
                act.activation(mT[:, g % 2, :], o[0:8, :], ACT.Copy).then_inc(mT_sb, 1)

            def evac_values(r, g):
                act.wait_ge(pv_ps, at(pv_ps, r, UNITS * (g + 1)))
                if g == 1:
                    act.wait_ge(ot3_ps, at(ot3_ps, r, 1))
                else:
                    act.wait_ge(ot_ps, at(ot_ps, r, g - 1 if g else 0))
                act.activation(oT[:, g % 2, :], R[0][:, :], ACT.Copy).then_inc(oT_sb, 1)

            def evac_y(r, c):
                act.wait_ge(yT_ps, at(yT_ps, r, c + 1))
                act.wait_ge(op_ps, at(op_ps, r, 1))
                for n in range(2):
                    i = act.activation(yT[:, n, c * P:(c + 1) * P], R[2][:, n * P:(n + 1) * P], ACT.Copy,
                                       scale=vec[:, V_NORM + n:V_NORM + n + 1])
                i.then_inc(yT_sb, 1)

            def evac_a(r):
                act.wait_ge(xaT_ps, at(xaT_ps, r, 1))
                act.wait_ge(z_ps, at(z_ps, r, T))
                act.activation(xaT[:], R[1][:, :], ACT.Identity, bias=vec[:, V_LN1B:V_LN1B + 1],
                               scale=vec[:, V_LN1W:V_LN1W + 1]).then_inc(xaT_sb, 1)

            def evac_b(r):
                act.wait_ge(xbT_ps, at(xbT_ps, r, 1))
                act.wait_ge(qkv_ps, at(qkv_ps, r, T))
                act.activation(xbT[:], R[1][:, :], ACT.Copy,
                               scale=vec[:, V_N1W:V_N1W + 1]).then_inc(xbT_sb, 1)

            def hidden(r, k, dst, func, bias=0.0):
                act.wait_ge(up_ps, at(up_ps, r, k + 1 if k < 15 else k))
                act.activation(dst, R[k % 4][:, :], func, bias=bias).then_inc(act_up, 1)

            def stage_b(r, tail, head):
                if head:
                    evac_qkv(r)
                    act.wait_ge(qkv_sb, at(qkv_sb, r, T))
                    act.activation(sq[:], qk[:], ACT.Square).then_inc(sq_sb, 1)
                    act.wait_ge(conv_dve, at(conv_dve, r, 0))
                    act.wait_ge(conv_pool, at(conv_pool, r, 0))
                    for n in range(3):
                        act.wait_ge(xbc_ps, at(xbc_ps, r, n + 1))
                        act.activation(xc[:, n, 3:L + 3], bank(n), ACT.Copy).then_inc(xc_sb, 1)
                if tail:
                    act.wait_ge(aoT_ps, at(aoT_ps, r, 1))
                    act.activation(aoT[:], R[0][:, :], ACT.Copy).then_inc(aoT_sb, 1)
                if head:
                    act.wait_ge(ssqk_sb, at(ssqk_sb, r, 2))
                    act.activation(rqk[:, 2], rqk[:, 1], ACT.Ln).then_inc(rqk_sb, 1)
                    act.wait_ge(rqk_sb, at(rqk_sb, r, 1))
                    act.activation(rqk[:, 0], rqk[:, 2], ACT.Exp, scale=-0.5).then_inc(rqk_sb, 1)
                    act.wait_ge(spa_sb, at(spa_sb, r, 0))
                    act.wait_ge(yz_sb, at(yz_sb, r, 0))
                    for n, t in enumerate((3, 0, 1, 2)):
                        act.wait_ge(z_ps, at(z_ps, r, n + 1))
                        act.activation(zraw[:, t, :], bank(t)[:, 0:DI + NH], ACT.Copy).then_inc(z_sb, 1)
                if tail:
                    act.wait_ge(x2_sb, at(x2_sb, r, 2))
                    act.wait_ge(r3_sb, at(r3_sb, r, 0))
                    act.wait_ge(yss_sb, at(yss_sb, r, 0))
                    for t in range(T):
                        i = act.activation(junk[:, t // 2, t % 2 * D:t % 2 * D + D], x2[:, t, :], ACT.Square,
                                           accum_out=x2ss[:, t:t + 1])
                    i.then_inc(x2ss_sb, 1)
                    act.wait_ge(x1T_ps, at(x1T_ps, r, 1))
                    act.activation(x1T[:], R[1][:, :], ACT.Identity, bias=vec[:, V_LN2B:V_LN2B + 1],
                                   scale=vec[:, V_LN2W:V_LN2W + 1]).then_inc(x1T_sb, 1)
                    act.wait_ge(xfT_ps, at(xfT_ps, r, 1))
                    act.activation(xfT[:], R[0][:, :], ACT.Copy,
                                   scale=vec[:, V_N2W:V_N2W + 1]).then_inc(xfT_sb, 1)
                if head:
                    act.wait_ge(spa_sb, at(spa_sb, r, 2))
                    act.activation(sp[:, 2], sp[:, 1], ACT.Exp, scale=-1.0).then_inc(spe_sb, 1)
                if tail:
                    act.wait_ge(gate_sb, at(gate_sb, r, 6))
                    act.wait_ge(wts_sb, at(wts_sb, r, 0))
                    act.activation(gt[:, 5], gt[:, 4], ACT.Exp).then_inc(gexp_sb, 1)
                if head:
                    act.wait_ge(e_ps, at(e_ps, r, 0))
                    for g in range(G):
                        act.wait_ge(qkT_ps, at(qkT_ps, r, 2 * g + 1))
                        act.activation(qT[:, g, :], bank(2 * g % 4), ACT.Copy).then_inc(qT_sb, 1)
                if tail:
                    act.wait_ge(moe_ps, at(moe_ps, r, 0))
                    act.wait_ge(pv_ps, at(pv_ps, r, 0))
                    act.wait_ge(seg_ps, at(seg_ps, r, 0))
                    act.wait_ge(wm_sb, at(wm_sb, r, 0))
                    hidden(r, 0, h0[:, 0], ACT.Gelu)
                    hidden(r, 1, h0[:, 1], ACT.Gelu)
                    hidden(r, 2, h3a[:], ACT.Gelu)
                    hidden(r, 3, h2a[:, 0], ACT.Gelu)
                    hidden(r, 4, h2a[:, 1], ACT.Gelu)
                    hidden(r, 5, hm[:, 0], ACT.Gelu, vec[:, V_B1:V_B1 + 1])
                    hidden(r, 6, hm[:, 1], ACT.Gelu, vec[:, V_B1 + 1:V_B1 + 2])
                    hidden(r, 7, h3b[:, 0], ACT.Gelu)
                    hidden(r, 8, h3b[:, 1], ACT.Gelu)
                    hidden(r, 9, h2b[:, 0], ACT.Gelu)
                    hidden(r, 10, h2b[:, 1], ACT.Gelu)
                    hidden(r, 11, hm[:, 2], ACT.Gelu, vec[:, V_B1 + 2:V_B1 + 3])
                    hidden(r, 12, hm[:, 3], ACT.Gelu, vec[:, V_B1 + 3:V_B1 + 4])
                    hidden(r, 13, h2c[:, 0], ACT.Gelu)
                    hidden(r, 14, h2c[:, 1], ACT.Gelu)
                if head:
                    evac_maxima(r, 0, R[3])
                    act.wait_ge(conv_dve, at(conv_dve, r, 2 * TAPS))
                    act.wait_ge(conv_pool, at(conv_pool, r, 2 * TAPS - 1))
                    act.wait_ge(y_ps, at(y_ps, r, 0))
                    act.wait_ge(c_moved, at(c_moved, r, 0))
                    act.activation(xact[:], cv[:], ACT.Silu).then_inc(conv_sb, 1)
                if tail:
                    act.wait_ge(h1_sb, at(h1_sb, r, 0))
                    act.wait_ge(y_ps, at(y_ps, r, 0))
                    hidden(r, 16, h1a[:, 0], ACT.Silu)
                    hidden(r, 17, h1a[:, 1], ACT.Silu)
                if head:
                    act.wait_ge(z_sb, at(z_sb, r, T))
                    act.wait_ge(spa_sb, at(spa_sb, r, 1))
                    act.activation(zs, zs, ACT.Silu).then_inc(zs_sb, 1)
                    evac_maxima(r, 1, R[1])

            def exponentiate(r, g, u):
                i, _ = unit(u)
                e = UNITS * g + u
                which = 1 if g < 2 else u % 2
                act.wait_ge(e_ps, at(e_ps, r, e + 1))
                act.wait_ge(pv_ps, at(pv_ps, r, e - 3))
                n = L - P * i
                act.activation(pr[:, e % 4, :, 0:n], S[which][:, :, 0:n], ACT.Exp).then_inc(p_sb, 1)

            def stage_a(r, tail):
                for g in range(G):
                    for u in range(UNITS):
                        exponentiate(r, g, u)
                        if u == 0:
                            if g == 0:
                                act.wait_ge(cum_ps, at(cum_ps, r, 1))
                                act.wait_ge(h_sb, at(h_sb, r, 0))
                                act.wait_ge(yc_sb, at(yc_sb, r, 0))
                                act.wait_ge(xw_sb, at(xw_sb, r, 0))
                                act.activation(dec[:].rearrange("p a c h -> p (a c h)"), R[1][:, 0:48],
                                               ACT.Exp).then_inc(dec_sb, 1)
                            else:
                                evac_values(r, g - 1)
                                evac_y(r, g - 1)
                            act.wait_ge(seg_ps, at(seg_ps, r, g + 1))
                            act.wait_ge(wm_sb, at(wm_sb, r, g - 1))
                            act.activation(es[:, g % 2].rearrange("p h t -> p (h t)"), R[1][:, :],
                                           ACT.Exp).then_inc(seg_sb, 1)
                        if u == 2 and g in (1, 2):
                            evac_maxima(r, g + 1, R[1])
                        if u == 5:
                            act.wait_ge(yz_sb, at(yz_sb, r, g + 1))
                            act.wait_ge(ry_sb, at(ry_sb, r, 1))
                            act.wait_ge(yss_sb, at(yss_sb, r, g - 1))
                            act.wait_ge(x2ss_sb, at(x2ss_sb, r, 1))
                            act.activation(junk[:, g % 2, :], yz[:, g % 2, :], ACT.Square,
                                           accum_out=yss[:, g:g + 1]).then_inc(yss_sb, 1)
                        if u == 6 and g == 0 and tail:
                            act.wait_ge(moe_sb, at(moe_sb, r, T * E))
                            act.wait_ge(og_sb, at(og_sb, r, 0))
                            act.activation(gs[:], x2[:], ACT.Silu).then_inc(gs_sb, 1)
                        if u == 5 and g == 3:
                            evac_a(r)
                evac_y(r, T - 1)
                evac_b(r)
                evac_values(r, G - 1)

            for sem in act_sems:
                act.sem_inc(sem, per[sem.name])
            for sem in (aoT_sb, x2ss_sb, xfT_sb, x1T_sb, gexp_sb, act_up, gs_sb):
                act.sem_inc(sem, per[sem.name])
            act.wait_ge(c_loaded, 48)
            act.activation(neg_a[:], row[:, R_ALOG:R_ALOG + NH], ACT.Exp).then_inc(act_set, 1)
            evac_a(-2)
            evac_b(-2)
            stage_b(-1, False, True)
            stage_a(-1, False)
            with act.Fori(0, B - 1) as r:
                stage_b(r, True, True)
                stage_a(r, True)
            stage_b(B - 1, True, False)
            act.wait_ge(moe_sb, at(moe_sb, B - 1, T * E))
            act.wait_ge(og_sb, at(og_sb, B - 1, 0))
            act.activation(gs[:], x2[:], ACT.Silu).then_inc(gs_sb, 1)

        @block.vector
        def _(dve):
            tt, ts, stt = dve.tensor_tensor, dve.tensor_scalar, dve.scalar_tensor_tensor

            def vcol(n):
                return vec[:, n:n + 1]

            def values(r, g, turned, done):
                view = R[3][:, :].rearrange("p (t j x) -> p t j x", t=T, j=4)
                dve.wait_ge(turned, at(turned, r, g + 1 if g < 3 else 1))
                dve.wait_ge(aoT_ps, at(aoT_ps, r, 1 if g < 3 else 0))
                dve.reciprocal(rden[:], view[:, :, :, HD]).then_inc(done, 1)
                dve.wait_ge(done, at(done, r, 2 * g + 1 if g < 3 else 1))
                tt(ao[:, :, 32 * g:32 * g + 32].rearrange("p t (j d) -> p t j d", j=4),
                   view[:, :, :, 0:HD], rden[:].unsqueeze(3).broadcast_to([P, T, 4, HD]),
                   ALU.mult).then_inc(done, 1)

            def maxima(r, g, u):
                i, pair = unit(u)
                which = u % 2 if g < 2 else 0
                dve.wait_ge(s_ps, at(s_ps, r, UNITS * g + u + 1))
                dve.tensor_reduce(mx[:, i, g, 2 * pair:2 * pair + 2], S[which][:, :, 0:P * (i + 1)],
                                  AX.X, ALU.max, negate=True).then_inc(mx_sb, 1)

            def split_maxima(r, g):
                dve.wait_ge(mx_sb, at(mx_sb, r, UNITS * (g + 1)))
                dve.wait_ge(mT_ps, at(mT_ps, r, g + 1 - G))
                dve.tensor_copy(mhl[:, g, :, :, 0].bitcast(F32R), mx[:, :, g, :]).then_inc(mhl_sb, 1)
                dve.wait_ge(mhl_sb, at(mhl_sb, r, 2 * g + 1))
                tt(mhl[:, g, :, :, 1], mx[:, :, g, :], mhl[:, g, :, :, 0],
                   ALU.subtract).then_inc(mhl_sb, 1)

            def conv_taps(r, n, taps):
                for k in taps:
                    wk = vcol(V_CONVW + TAPS * n + k)
                    if k == TAPS - 1:
                        ts(cv[:, n], xc[:, n, k:k + L], wk, vcol(V_CONVB + n), ALU.mult,
                           ALU.add).then_inc(conv_dve, 1)
                    else:
                        dve.wait_ge(conv_dve, at(conv_dve, r, TAPS * n + 3 - k))
                        stt(out=cv[:, n], in0=xc[:, n, k:k + L], scalar=wk, in1=cv[:, n],
                            op0=ALU.mult, op1=ALU.add).then_inc(conv_dve, 1)

            def stats(r):
                dve.wait_ge(x_loaded, at(x_loaded, r, 16))
                for t in range(T):
                    i = dve.bn_stats(st6[:, t, :], xin[:, t, :])
                i.then_inc(stat_sb, 1)
                dve.wait_ge(stat_sb, at(stat_sb, r, 1))
                dve.sem_inc(dve_passed, 1)
                for t in range(T):
                    i = dve.bn_aggr(mv[:, t, :], st6[:, t, :])
                i.then_inc(stat_sb, 1)

            def norms(r):
                dve.wait_ge(rn_sb, at(rn_sb, r, 8))
                dve.wait_ge(xaT_ps, at(xaT_ps, r, 0))
                dve.wait_ge(xbT_ps, at(xbT_ps, r, 0))
                for t in range(T):
                    ts(xa[:, t, :], xin[:, t, :], mv[:, t, 0:1], lnv[:, 4, t:t + 1], ALU.subtract, ALU.mult)
                for t in range(T):
                    i = ts(xb[:, t, :], xin[:, t, :], mv[:, t, 0:1], lnv[:, 5, t:t + 1],
                           ALU.subtract, ALU.mult)
                i.then_inc(xab_sb, 1)

            def gate_logits(r):
                flat = [gt[:, n].rearrange("p t e -> p (t e)") for n in range(12)]
                dve.wait_ge(gate_ps, at(gate_ps, r, 1))
                dve.tensor_copy(flat[0], R[2][:, 0:T * E]).then_inc(gate_sb, 1)
                dve.wait_ge(gate_sb, at(gate_sb, r, 1))
                tt(flat[1], flat[0], flat[0], ALU.is_equal).then_inc(gate_sb, 1)
                ts(flat[2], flat[0], FMAX, -FMAX, ALU.min, ALU.max).then_inc(gate_sb, 1)
                dve.wait_ge(gate_sb, at(gate_sb, r, 3))
                tt(flat[3], flat[2], flat[1], ALU.mult).then_inc(gate_sb, 1)
                dve.wait_ge(gate_sb, at(gate_sb, r, 4))
                dve.tensor_reduce(g1[:, 0, :], gt[:, 3], AX.X, ALU.max).then_inc(gate_sb, 1)
                dve.wait_ge(gate_sb, at(gate_sb, r, 5))
                tt(gt[:, 4], gt[:, 3], g1[:, 0, :].unsqueeze(2).broadcast_to([P, T, E]),
                   ALU.subtract).then_inc(gate_sb, 1)

            def gate_weights(r):
                prob = gt[:, 6]
                dve.wait_ge(gexp_sb, at(gexp_sb, r, 1))
                dve.tensor_reduce(g1[:, 1, :], gt[:, 5], AX.X, ALU.add).then_inc(wts_sb, 1)
                dve.wait_ge(wts_sb, at(wts_sb, r, 1))
                dve.reciprocal(g1[:, 2, :], g1[:, 1, :]).then_inc(wts_sb, 1)
                dve.wait_ge(wts_sb, at(wts_sb, r, 2))
                tt(prob, gt[:, 5], g1[:, 2, :].unsqueeze(2).broadcast_to([P, T, E]),
                   ALU.mult).then_inc(wts_sb, 1)
                dve.wait_ge(wts_sb, at(wts_sb, r, 3))
                other = prob.unsqueeze(2).broadcast_to([P, T, E, E])
                own = prob.unsqueeze(3).broadcast_to([P, T, E, E])
                tt(gq[:, 0], other, own, ALU.is_gt).then_inc(wts_sb, 1)
                tt(gq[:, 1], other, own, ALU.is_equal).then_inc(wts_sb, 1)
                dve.wait_ge(wts_sb, at(wts_sb, r, 5))
                tt(gq[:, 1], gq[:, 1], before.unsqueeze(1).broadcast_to([P, T, E, E]),
                   ALU.mult).then_inc(wts_sb, 1)
                dve.wait_ge(wts_sb, at(wts_sb, r, 6))
                tt(gq[:, 0], gq[:, 0], gq[:, 1], ALU.add).then_inc(wts_sb, 1)
                dve.wait_ge(wts_sb, at(wts_sb, r, 7))
                dve.tensor_reduce(gt[:, 7], gq[:, 0], AX.X, ALU.add).then_inc(wts_sb, 1)
                dve.wait_ge(wts_sb, at(wts_sb, r, 8))
                stt(out=gt[:, 8], in0=gt[:, 7], scalar=1.5, in1=prob, op0=ALU.is_lt,
                    op1=ALU.mult).then_inc(wts_sb, 1)
                dve.wait_ge(wts_sb, at(wts_sb, r, 9))
                dve.tensor_reduce(g1[:, 3, :], gt[:, 8], AX.X, ALU.add).then_inc(wts_sb, 1)
                dve.wait_ge(wts_sb, at(wts_sb, r, 10))
                ts(g1[:, 1, :], g1[:, 3, :], 1e-8, None, ALU.add).then_inc(wts_sb, 1)
                dve.wait_ge(wts_sb, at(wts_sb, r, 11))
                dve.reciprocal(g1[:, 2, :], g1[:, 1, :]).then_inc(wts_sb, 1)
                dve.wait_ge(wts_sb, at(wts_sb, r, 12))
                tt(wts[:], gt[:, 8], g1[:, 2, :].unsqueeze(2).broadcast_to([P, T, E]),
                   ALU.mult).then_inc(wts_sb, 1)

            def time_steps(r):
                dve.wait_ge(spe_sb, at(spe_sb, r, 1))
                ts(sp[:, 3], sp[:, 2], 2.0, None, ALU.add).then_inc(dt_sb, 1)
                dve.wait_ge(dt_sb, at(dt_sb, r, 1))
                dve.reciprocal(sp[:, 4], sp[:, 3]).then_inc(dt_sb, 1)
                dve.wait_ge(dt_sb, at(dt_sb, r, 2))
                tt(sp[:, 5], sp[:, 2], sp[:, 4], ALU.mult).then_inc(dt_sb, 1)
                dve.wait_ge(dt_sb, at(dt_sb, r, 3))
                tt(sp[:, 6], sp[:, 5], sp[:, 5], ALU.mult).then_inc(dt_sb, 1)
                dve.wait_ge(dt_sb, at(dt_sb, r, 4))
                ts(sp[:, 7], sp[:, 6], 1.0 / 15, None, ALU.mult).then_inc(dt_sb, 1)
                for n, c in enumerate((13, 11, 9, 7, 5, 3)):
                    dve.wait_ge(dt_sb, at(dt_sb, r, 5 + n))
                    stt(out=sp[:, 7], in0=sp[:, 7], scalar=1.0 / c, in1=sp[:, 6], op0=ALU.add,
                        op1=ALU.mult).then_inc(dt_sb, 1)
                dve.wait_ge(dt_sb, at(dt_sb, r, 11))
                stt(out=sp[:, 8], in0=sp[:, 7], scalar=1.0, in1=sp[:, 5], op0=ALU.add,
                    op1=ALU.mult).then_inc(dt_sb, 1)
                ts(sp[:, 9], sp[:, 0], 0.0, None, ALU.max).then_inc(dt_sb, 1)
                dve.wait_ge(dt_sb, at(dt_sb, r, 13))
                stt(out=dt[:], in0=sp[:, 8], scalar=2.0, in1=sp[:, 9], op0=ALU.mult,
                    op1=ALU.add).then_inc(dt_sb, 1)
                dve.wait_ge(dt_sb, at(dt_sb, r, 14))
                dve.wait_ge(cum_ps, at(cum_ps, r, 0))
                dve.wait_ge(rs_sb, at(rs_sb, r, 0))
                tt(dta[:], dt[:], neg_a[:].unsqueeze(1).broadcast_to([P, T, NH]),
                   ALU.mult).then_inc(dt_sb, 1)

            def stage_b(r, tail, head):
                if tail:
                    values(r, 3, ot3_ps, ao3_sb)
                    dve.wait_ge(op_ps, at(op_ps, r, 1))
                    dve.wait_ge(ry_sb, at(ry_sb, r, 2))
                    dve.wait_ge(xn_sb, at(xn_sb, r, 0))
                    dve.wait_ge(og_sb, at(og_sb, r, 0))
                    for t in range(T):
                        stt(out=x1[:, t, :], in0=R[2][:, t * P:(t + 1) * P], scalar=ry[:, 1, t:t + 1],
                            in1=xn[:, t, :], op0=ALU.mult, op1=ALU.add).then_inc(x1_sb, 1)
                if head:
                    dve.wait_ge(sq_sb, at(sq_sb, r, 1))
                    dve.tensor_reduce(rqk[:, 0], sq[:].rearrange("p t a h d -> p (t a h) d"), AX.X,
                                      ALU.add).then_inc(ssqk_sb, 1)
                    dve.wait_ge(ssqk_sb, at(ssqk_sb, r, 1))
                    ts(rqk[:, 1], rqk[:, 0], 1.0 / HD, EPS_RMS, ALU.mult, ALU.add).then_inc(ssqk_sb, 1)
                if tail:
                    dve.wait_ge(x1_sb, at(x1_sb, r, T))
                    for t in range(T):
                        i = dve.bn_stats(st2[:, t, :], x1[:, t, :])
                    i.then_inc(ln2_sb, 1)
                    dve.wait_ge(ln2_sb, at(ln2_sb, r, 1))
                    dve.sem_inc(dve_passed, 1)
                    for t in range(T):
                        i = dve.bn_aggr(mv2[:, t, :], st2[:, t, :])
                    i.then_inc(ln2_sb, 1)
                    dve.wait_ge(wo_ps, at(wo_ps, r, 1))
                    dve.wait_ge(gs_sb, at(gs_sb, r, 0))
                    tt(x2[:, :, MASKED:D], R[3][:, 0:T * OC].rearrange("p (t c) -> p t c", t=T),
                       xn[:, :, MASKED:D], ALU.add).then_inc(x2_sb, 1)
                    dve.tensor_copy(x2[:, :, 0:MASKED], xn[:, :, 0:MASKED]).then_inc(x2_sb, 1)
                if head:
                    dve.wait_ge(rqk_sb, at(rqk_sb, r, 2))
                    tt(sq[:].rearrange("p t a h d -> p (t a h) d"),
                       qk[:].rearrange("p t a h d -> p (t a h) d"),
                       rqk[:, 0].unsqueeze(2).broadcast_to([P, T * 2 * AH, HD]),
                       ALU.mult).then_inc(nqk_sb, 1)
                if tail:
                    dve.wait_ge(r2_sb, at(r2_sb, r, 2))
                    for t in range(T):
                        i = ts(x1n[:, t, :], x1[:, t, :], mv2[:, t, 0:1], r2[:, 1, t:t + 1],
                               ALU.subtract, ALU.mult)
                    i.then_inc(x1n_sb, 1)
                if head:
                    dve.wait_ge(nqk_sb, at(nqk_sb, r, 1))
                    flat = sq[:].rearrange("p t a h d -> p t (a h d)")
                    tt(flat, flat, wqk[:].rearrange("p a h d -> p (a h d)").unsqueeze(1)
                       .broadcast_to([P, T, 2 * D]), ALU.mult).then_inc(nqk_sb, 1)
                    dve.wait_ge(nqk_sb, at(nqk_sb, r, 2))
                    dve.wait_ge(qkT_ps, at(qkT_ps, r, 0))
                    dve.tensor_copy(tokqk[:, :, :, :, 0:HD].rearrange("p t a h d -> p (t a h) d").bitcast(F32R),
                                    sq[:].rearrange("p t a h d -> p (t a h) d")).then_inc(nqk_sb, 1)
                    dve.wait_ge(nqk_sb, at(nqk_sb, r, 3))
                    tt(tokqk[:, :, 0, :, 2 * HD:3 * HD], sq[:, :, 0], tokqk[:, :, 0, :, 0:HD], ALU.subtract)
                    tt(tokqk[:, :, 1, :, HD:2 * HD], sq[:, :, 1], tokqk[:, :, 1, :, 0:HD],
                       ALU.subtract).then_inc(lo_sb, 1)
                if tail:
                    dve.wait_ge(r3_sb, at(r3_sb, r, 2))
                    for t in range(T):
                        i = ts(xf[:, t, :], x2[:, t, :], r3[:, 1, t:t + 1], None, ALU.mult)
                    i.then_inc(xf_sb, 1)
                if head:
                    dve.wait_ge(z_sb, at(z_sb, r, T))
                    tt(sp[:, 0], zraw[:, :, DI:DI + NH],
                       row[:, R_DTB:R_DTB + NH].unsqueeze(1).broadcast_to([P, T, NH]),
                       ALU.add).then_inc(spa_sb, 1)
                    dve.wait_ge(spa_sb, at(spa_sb, r, 1))
                    stt(out=sp[:, 1], in0=sp[:, 0], scalar=-1.0, in1=sp[:, 0], op0=ALU.mult,
                        op1=ALU.max).then_inc(spa_sb, 1)
                if tail:
                    gate_logits(r)
                if head:
                    dve.wait_ge(e_ps, at(e_ps, r, 0))
                    for g in range(G):
                        dve.wait_ge(qkT_ps, at(qkT_ps, r, 2 * g + 2))
                        dve.tensor_copy(kT[:, g, :], bank((2 * g + 1) % 4)).then_inc(kT_sb, 1)
                    dve.wait_ge(xc_sb, at(xc_sb, r, 3))
                    dve.wait_ge(conv_sb, at(conv_sb, r, 0))
                    for m in range(2 * UNITS):
                        maxima(r, m // UNITS, m % UNITS)
                        if m == 0:
                            conv_taps(r, 0, (3, 2))
                        if m == 1:
                            conv_taps(r, 0, (1, 0))
                        if m == 2:
                            conv_taps(r, 1, (3, 2))
                        if m == 3:
                            conv_taps(r, 1, (1, 0))
                        if m == 4:
                            time_steps(r)
                        if m == UNITS - 1:
                            split_maxima(r, 0)
                        if m == UNITS + 1 and tail:
                            gate_weights(r)
                        if m == 2 * UNITS - 1:
                            split_maxima(r, 1)
                elif tail:
                    gate_weights(r)
                if tail:
                    dve.wait_ge(moe_ps, at(moe_ps, r, 0))
                    for n in range(2):
                        dve.wait_ge(up_ps, at(up_ps, r, 18 + n))
                        dve.wait_ge(act_up, at(act_up, r, 16 + n))
                        tt(h1[:, n], R[(18 + n) % 4][:, :], h1a[:, n], ALU.mult).then_inc(h1_sb, 1)
                    dve.wait_ge(mlp_ps, at(mlp_ps, r, 1))
                    dve.wait_ge(x1b_sb, at(x1b_sb, r, 1))
                    tt(x1[:], R[0][:, :].rearrange("p (t c) -> p t c", t=T), x1[:],
                       ALU.add).then_inc(sv_sb, 1)
                    for t in range(T):
                        dve.wait_ge(moe_ps, at(moe_ps, r, t + 1))
                        for e in range(E):
                            if e:
                                dve.wait_ge(moe_sb, at(moe_sb, r, E * t + e))
                            else:
                                dve.wait_ge(wts_sb, at(wts_sb, r, 13))
                            stt(out=x2[:, t, MASKED:D], in0=R[(22 + t) % 4][:, e * OC:(e + 1) * OC],
                                scalar=wts[:, t, e:e + 1],
                                in1=x2[:, t, MASKED:D],
                                op0=ALU.mult, op1=ALU.add).then_inc(moe_sb, 1)

            def scan_products(r, c):
                dve.wait_ge(xt_ps, at(xt_ps, r, c + 1))
                dve.wait_ge(y_ps, at(y_ps, r, c - 1))
                dve.wait_ge(xw_sb, at(xw_sb, r, c - 1 if c >= 2 else 0))
                dve.wait_ge(hn_ps, at(hn_ps, r, c - 1 if c >= 2 else 0))
                tt(xdt[:, c % 2, :].rearrange("p (h d) -> p h d", h=NH),
                   R[2][:, 0:DI].rearrange("p (h d) -> p h d", h=NH),
                   dt[:, c, :].unsqueeze(2).broadcast_to([P, NH, HP]), ALU.mult).then_inc(xdt_sb, 1)
                dve.tensor_copy(btok[:, c % 2, :], R[2][:, DI:DI + NS])
                tt(gm[:, c % 2, :], R[2][:, 3 * P:4 * P], upto, ALU.mult).then_inc(gm_sb, 1)

            def scan_weights(r, c):
                dve.wait_ge(seg_sb, at(seg_sb, r, c + 1))
                dve.wait_ge(gm_sb, at(gm_sb, r, c + 1))
                dve.wait_ge(y_ps, at(y_ps, r, c - 1))
                tt(wm[:, c % 2], es[:, c % 2], gm[:, c % 2, :].unsqueeze(1).broadcast_to([P, NH, P]),
                   ALU.mult).then_inc(wm_sb, 1)

            def scan_combine(r, c):
                dve.wait_ge(y_ps, at(y_ps, r, c + 1))
                dve.wait_ge(zs_sb, at(zs_sb, r, 1))
                dve.wait_ge(yT_ps, at(yT_ps, r, c - 1))
                dve.wait_ge(yss_sb, at(yss_sb, r, c - 1))
                if c == 0:
                    y = R[3][:, 0:DI]
                else:
                    tt(yc[:, 0, :].rearrange("p (h d) -> p h d", h=NH),
                       R[3][:, DI:2 * DI].rearrange("p (h d) -> p h d", h=NH),
                       dec[:, 0, c, :].unsqueeze(2).broadcast_to([P, NH, HP]), ALU.mult)\
                        .then_inc(yc_sb, 1)
                    dve.wait_ge(yc_sb, at(yc_sb, r, 2 * c - 1))
                    tt(yc[:, 1, :], R[3][:, 0:DI], yc[:, 0, :], ALU.add).then_inc(yc_sb, 1)
                    dve.wait_ge(yc_sb, at(yc_sb, r, 2 * c))
                    y = yc[:, 1, :]
                tt(yz[:, c % 2, :], y, zraw[:, c, 0:DI], ALU.mult).then_inc(yz_sb, 1)

            def scan_state(r, c):
                dve.wait_ge(hn_ps, at(hn_ps, r, c + 1))
                if c == 0:
                    dve.tensor_copy(hst[:], R[1][0:NS, 0:DI]).then_inc(h_sb, 1)
                else:
                    tt(hdec[:].rearrange("p (h d) -> p h d", h=NH),
                       hst[:].rearrange("p (h d) -> p h d", h=NH),
                       dec[0:NS, 2, c, :].unsqueeze(2).broadcast_to([NS, NH, HP]),
                       ALU.mult).then_inc(h_sb, 1)
                    dve.wait_ge(h_sb, at(h_sb, r, 2 * c))
                    tt(hst[:], R[1][0:NS, 0:DI], hdec[:], ALU.add).then_inc(h_sb, 1)

            def stage_a(r):
                dve.wait_ge(rn_sb, at(rn_sb, r, 0))
                for t in range(T):
                    i = ts(xn[:, t, :], xin[:, t, :], mv[:, t, 0:1], lnv[:, 1, t:t + 1],
                           ALU.subtract, ALU.mult)
                i.then_inc(xn_sb, 1)
                for g in range(G):
                    for u in range(UNITS):
                        if g < 2:
                            maxima(r, g + 2, u)
                        if u == 0:
                            scan_products(r, g)
                        if u == 1:
                            scan_weights(r, g)
                        if u == 2 and g >= 1:
                            values(r, g - 1, ot_ps, ao_sb)
                        if u == 4:
                            scan_combine(r, g)
                        if u == 5 and g < T - 1:
                            scan_state(r, g)
                        if u == 6 and g == 1:
                            stats(r)
                        if u == 5 and g == 2:
                            norms(r)
                    if g < 2:
                        split_maxima(r, g + 2)

            for sem in dve_sems:
                dve.sem_inc(sem, per[sem.name])
            for sem in (ao3_sb, x1_sb, ln2_sb, x2_sb, xf_sb, x1n_sb, gate_sb, wts_sb, h1_sb, sv_sb, moe_sb):
                dve.sem_inc(sem, per[sem.name])
            stats(-2)
            dve.wait_ge(c_loaded, 48)
            dve.tensor_copy(identb[:], ident).then_inc(dve_set, 1)
            dve.tensor_copy(maskb[:], future).then_inc(dve_set, 1)
            for n, (col, scale) in enumerate(((R_QN, HD ** -0.5), (R_KN, 1.0))):
                ts(wqk[:, n], row[:, col:col + HD].unsqueeze(1).broadcast_to([P, AH, HD]), scale, None,
                   ALU.mult).then_inc(dve_set, 1)
            for n in range(2):
                ts(diag_d[:, n, :], ident, vcol(V_DCH + n), None, ALU.mult).then_inc(dve_set, 1)
            dve.wait_ge(act_set, 1)
            ts(neg_a[:], neg_a[:], -1.0, None, ALU.mult).then_inc(dve_set, 1)
            norms(-2)
            dve.wait_ge(dve_set, 7)
            stage_b(-1, False, True)
            stage_a(-1)
            with dve.Fori(0, B - 1) as r:
                stage_b(r, True, True)
                stage_a(r)
            stage_b(B - 1, True, False)

        @block.gpsimd
        def _(pool):
            tt, ts = pool.tensor_tensor, pool.tensor_scalar

            def inverse_root(r, src, steps, sig, scale, eps):
                ts(steps[:, 0, :], src, scale, eps, ALU.mult, ALU.add).then_inc(sig, 1)
                pool.wait_ge(sig, at(sig, r, 1))
                tt(steps[:, 1, :], steps[:, 0, :], minus_half[:, 0:T], ALU.pow).then_inc(sig, 1)

            def first_norms(r):
                var = mv[:, :, 1]
                pool.wait_ge(stat_sb, at(stat_sb, r, 2))
                pool.wait_ge(xn_sb, at(xn_sb, r, 1))
                pool.wait_ge(xab_sb, at(xab_sb, r, 0))
                pool.sem_inc(pool_passed, 1)
                ts(lnv[:, 0, :], var, 1.0, EPS, ALU.mult, ALU.add).then_inc(rn_sb, 1)
                pool.wait_ge(rn_sb, at(rn_sb, r, 1))
                tt(lnv[:, 1, :], lnv[:, 0, :], minus_half[:, 0:T], ALU.pow).then_inc(rn_sb, 1)
                pool.wait_ge(rn_sb, at(rn_sb, r, 2))
                tt(lnv[:, 2, :], lnv[:, 1, :], lnv[:, 1, :], ALU.mult).then_inc(rn_sb, 1)
                pool.wait_ge(rn_sb, at(rn_sb, r, 3))
                tt(lnv[:, 3, :], lnv[:, 2, :], var, ALU.mult).then_inc(rn_sb, 1)
                pool.wait_ge(rn_sb, at(rn_sb, r, 4))
                pool.sem_inc(pool_passed, 1)
                ts(lnv[:, 4, :], lnv[:, 3, :], 1.0, EPS, ALU.mult, ALU.add).then_inc(rn_sb, 1)
                ts(lnv[:, 5, :], lnv[:, 3, :], 1.0, EPS_RMS, ALU.mult, ALU.add).then_inc(rn_sb, 1)
                pool.wait_ge(rn_sb, at(rn_sb, r, 6))
                tt(lnv[:, 6:8, :].rearrange("p a t -> p (a t)"), lnv[:, 4:6, :].rearrange("p a t -> p (a t)"),
                   minus_half[:], ALU.pow).then_inc(rn_sb, 1)
                pool.wait_ge(rn_sb, at(rn_sb, r, 7))
                tt(lnv[:, 4:6, :], lnv[:, 6:8, :], lnv[:, 1, :].unsqueeze(1).broadcast_to([P, 2, T]),
                   ALU.mult).then_inc(rn_sb, 1)

            def stage_b(r, tail, head):
                if tail:
                    pool.wait_ge(yss_sb, at(yss_sb, r, 0))
                    pool.wait_ge(x1_sb, at(x1_sb, r, 0))
                    pool.sem_inc(pool_passed, 1)
                    inverse_root(r, yss[:], ry, ry_sb, 1.0 / DI, EPS)
                    pool.wait_ge(ln2_sb, at(ln2_sb, r, 2))
                    pool.sem_inc(pool_passed, 1)
                    inverse_root(r, mv2[:, :, 1], r2, r2_sb, 1.0, EPS)
                    pool.wait_ge(x2ss_sb, at(x2ss_sb, r, 1))
                    pool.sem_inc(pool_passed, 1)
                    inverse_root(r, x2ss[:], r3, r3_sb, 1.0 / D, EPS_RMS)
                    pool.wait_ge(x1n_sb, at(x1n_sb, r, 1))
                    tt(x1[:], x1[:], row[:, R_B2:R_B2 + D].unsqueeze(1).broadcast_to([P, T, D]),
                       ALU.add).then_inc(x1b_sb, 1)
                if head:
                    pool.wait_ge(nqk_sb, at(nqk_sb, r, 3))
                    pool.wait_ge(qkT_ps, at(qkT_ps, r, 0))
                    pool.sem_inc(pool_passed, 1)
                    pool.tensor_copy(tokqk[:, :, 0, :, HD:2 * HD], tokqk[:, :, 0, :, 0:HD])
                    pool.tensor_copy(tokqk[:, :, 1, :, 2 * HD:3 * HD],
                                     tokqk[:, :, 1, :, 0:HD]).then_inc(dup_sb, 1)
                if head:
                    pool.wait_ge(xc_sb, at(xc_sb, r, 3))
                    pool.wait_ge(conv_sb, at(conv_sb, r, 0))
                    pool.sem_inc(pool_passed, 1)
                    n = 2
                    ts(cv[:, n], xc[:, n, 3:3 + L], vec[:, V_CONVW + 4 * n + 3:V_CONVW + 4 * n + 4],
                       vec[:, V_CONVB + n:V_CONVB + n + 1], ALU.mult, ALU.add).then_inc(conv_pool, 1)
                    for i, k in enumerate((2, 1, 0)):
                        tap = V_CONVW + 4 * n + k
                        if i:
                            pool.wait_ge(conv_pool, at(conv_pool, r, 2 * i + 1))
                            pool.sem_inc(pool_passed, 1)
                        ts(cm[:], xc[:, n, k:k + L], vec[:, tap:tap + 1], 0.0, ALU.mult,
                           ALU.add).then_inc(conv_pool, 1)
                        pool.wait_ge(conv_pool, at(conv_pool, r, 2 * i + 2))
                        tt(cv[:, n], cv[:, n], cm[:], ALU.add).then_inc(conv_pool, 1)

            def decays(r, c, tail):
                pool.wait_ge(dt_sb, at(dt_sb, r, 15))
                if c == 0 and tail:
                    pool.wait_ge(up_ps, at(up_ps, r, 11))
                pool.wait_ge(seg_ps, at(seg_ps, r, c - 1))
                tt(rs[:, c % 2], upto.unsqueeze(1).broadcast_to([P, NH, P]),
                   dta[:, c, :].unsqueeze(2).broadcast_to([P, NH, P]), ALU.mult).then_inc(rs_sb, 1)

            def join(r):
                pool.wait_ge(gs_sb, at(gs_sb, r, 1))
                pool.wait_ge(sv_sb, at(sv_sb, r, 1))
                tt(gs[:], x1[:], gs[:], ALU.mult).then_inc(og_sb, 1)
                pool.wait_ge(og_sb, at(og_sb, r, 1))
                pool.wait_ge(xres_loaded, at(xres_loaded, r, 16))
                tt(xres[:], gs[:], xres[:], ALU.add).then_inc(og_sb, 1)

            def stage_a(r, tail):
                decays(r, 0, tail)
                for g in range(G):
                    for u in range(UNITS):
                        e = UNITS * g + u
                        pool.wait_ge(p_sb, at(p_sb, r, e + 1))
                        pool.sem_inc(pool_passed, 1)
                        keep = pr[:, e % 4, :, 0:P]
                        pool.affine_select(out=keep, in_=keep, compare_op=ALU.is_ge, fill=0.0, base=0,
                                           pattern=[[0, 2], [1, P]], channel_multiplier=-1)\
                            .then_inc(pm_sb, 1)
                        if u == 1 and g < T - 1:
                            pool.wait_ge(xdt_sb, at(xdt_sb, r, g + 1))
                            pool.wait_ge(dec_sb, at(dec_sb, r, 1))
                            pool.wait_ge(hn_ps, at(hn_ps, r, g - 1 if g >= 2 else 0))
                            tt(xw[:, g % 2, :].rearrange("p (h d) -> p h d", h=NH),
                               xdt[:, g % 2, :].rearrange("p (h d) -> p h d", h=NH),
                               dec[:, 1, g, :].unsqueeze(2).broadcast_to([P, NH, HP]),
                               ALU.mult).then_inc(xw_sb, 1)
                        if u == 4 and g < T - 1:
                            decays(r, g + 1, tail)
                        if u == 0 and g == 1 and tail:
                            join(r)
                        if u == 1 and g == 2:
                            first_norms(r)

            for sem in pool_sems:
                pool.sem_inc(sem, per[sem.name])
            for sem in (ry_sb, r2_sb, r3_sb, x1b_sb, og_sb):
                pool.sem_inc(sem, per[sem.name])
            pool.memset(minus_half[:], -0.5).then_inc(pool_set, 1)
            pool.memset(va[:], 0.0).then_inc(pool_set, 1)
            pool.memset(tokqk[:], 0.0).then_inc(pool_set, 1)
            pool.memset(xc[:, :, 0:3], 0.0).then_inc(pool_set, 1)
            pool.wait_ge(pool_set, 3)
            pool.memset(va[:, :, :, HD:HD + 1], 1.0).then_inc(pool_set, 1)
            pool.memset(tokqk[:, :, 1, :, 3 * HD:3 * HD + 2], 1.0).then_inc(pool_set, 1)
            pool.wait_ge(c_loaded, 48)
            first_norms(-2)
            stage_b(-1, False, True)
            stage_a(-1, False)
            with pool.Fori(0, B - 1) as r:
                stage_b(r, True, True)
                stage_a(r, True)
            stage_b(B - 1, True, False)
            join(B - 1)


def kernel(**inputs):
    import numpy as np
    import concourse.bacc as bacc
    from concourse.bass_utils import run_bass_kernel_spmd

    a = {k.removeprefix("L0_"): np.asarray(v) for k, v in inputs.items()}
    f32 = np.float32

    def halves(m, n):
        return np.concatenate([m[i * P:(i + 1) * P] for i in range(n)], axis=1)

    proj = a["attn_in_proj_w"].T
    blocks = {
        "qkv": np.concatenate([a["ffn_wq"].T, a["ffn_wk"].T, a["ffn_wv"].T], axis=1),
        "x": proj[:, DI:DI + CONV],
        "zdt": np.concatenate([proj[:, 0:DI], proj[:, DI + CONV:]], axis=1),
        "wo": a["ffn_wo"].T[:, MASKED:],
        "op": halves(a["attn_out_proj_w"].T, 2),
        "gate": a["ffn_gate_w"].T,
        "e0u": a["ffn_e0_up"].T,
        "e3a": a["ffn_e3_down"].T,
        "e2a": a["ffn_e2_l1"].T,
        "w1": a["attn_mlp_w1"].T,
        "e3b": a["ffn_e3_up"].T,
        "e2b": halves(a["ffn_e2_l2"].T, 2),
        "e2c": halves(a["ffn_e2_l3"].T, 2),
        "e1a": a["ffn_e1_w1"].T,
        "e1b": a["ffn_e1_w2"].T,
        "w2": halves(a["attn_mlp_w2"].T, 4),
        "e0d": halves(a["ffn_e0_down"].T[:, MASKED:], 2),
        "e1d": halves(a["ffn_e1_down"].T[:, MASKED:], 2),
        "e2d": halves(a["ffn_e2_l4"].T[:, MASKED:], 2),
        "e3d": halves(a["ffn_e3_out"].T[:, MASKED:], 2),
    }
    weights = np.ascontiguousarray(np.concatenate([blocks[n] for n in W_COLS], axis=1))

    def cols(v, n=1):
        return v.reshape(n, P).T

    vectors = np.ascontiguousarray(np.concatenate([
        cols(a["attn_ln1_w"]), cols(a["attn_ln1_b"]), cols(a["ffn_n1_w"]), cols(a["attn_ln2_w"]),
        cols(a["attn_ln2_b"]), cols(a["ffn_n2_w"]), cols(a["attn_mlp_b1"], 4), cols(a["attn_norm_w"], 2),
        cols(a["attn_conv_b"], 3), halves(a["attn_conv_w"], 3), cols(np.repeat(a["attn_D"], HP), 2)], axis=1))
    rows = np.ascontiguousarray(np.broadcast_to(np.concatenate([
        a["attn_dt_bias"], a["attn_A_log"], a["ffn_qn_w"], a["ffn_kn_w"], a["attn_mlp_b2"]]), (P, R_TOTAL)))
    at = np.arange(P)
    consts = np.concatenate([
        np.eye(P), at[:, None] <= at, at[:, None] > at, np.ones((P, P)), np.where(at > at[:, None], NEG, 0.0),
        np.broadcast_to((np.arange(E) < np.arange(E)[:, None]).reshape(1, E * E), (P, E * E))],
        axis=1).astype(f32)

    nc = bacc.Bacc("TRN2", target_bir_lowering=False, num_devices=1)
    arrays = {"x": np.ascontiguousarray(a["attn_x"]), "weights": weights, "vectors": vectors, "rows": rows,
              "consts": consts}
    aps = [nc.dram_tensor(n, v.shape, mybir.dt.from_np(v.dtype), kind="ExternalInput").ap()
           for n, v in arrays.items()]
    out = nc.dram_tensor("out", (B, L, D), F32, kind="ExternalOutput").ap()
    build(nc, *aps, out)
    r = run_bass_kernel_spmd(nc, [arrays], core_ids=[0])
    return r.results[0]["out"]
```

```python
from contextlib import ExitStack

import concourse.bass as bass
from concourse import mybir

F32 = mybir.dt.float32
F32R = mybir.dt.float32r
BF16 = mybir.dt.bfloat16
ALU = mybir.AluOpType
ACT = mybir.ActivationFunctionType
AX = mybir.AxisListType

P = 128
B, L, D = 8, 512, 128
T = L // P
NH, HP, NS = 4, 64, 64
DI = NH * HP
CONV = DI + 2 * NS
TAPS = 4
AH, HD = 16, 8
G = 4
E = 4
MASKED = 32
OC = D - MASKED
EPS = 1e-5
EPS_RMS = 1.1920929e-07
FMAX = 3.4028234663852886e38
NEG = -1e30
EXP_LN = "natural_log_exp_and_others"
UNIT = ((512, 512, (0, 1)), (512, 512, (2, 3)), (384, 512, (0, 1)), (384, 512, (2, 3)),
        (256, 256, (0, 1, 2, 3)), (128, 256, (0, 1, 2, 3)))
UNITS = len(UNIT)
MAX_AT = {0: 12, 1: 13, 2: 14, 3: 15, 4: 16, 5: 17, 8: 18, 9: 19, 10: 20, 11: 21, 12: 22, 13: 23}
LAST_MAX = max(MAX_AT)
TAP_AT = {0: (0, 2), 2: (0, 1), 4: (0, 0), 6: (1, 2), 7: (1, 1), 8: (1, 0)}
WEIGHTS_FROM = 5
SIGMOID_AT = (8, 10, 13, 14, 15)
JOIN_AT = (16, 17, 19)
STATS_AT = 14
NORM_AT = (15, 16, 17)

W_COLS = {}
_at = 0
for _name, _n in (("qkv", 3 * D), ("x", CONV), ("zdt", DI + NH), ("wo", OC), ("op", 2 * D),
                  ("gate", E), ("e0u", 256), ("e3a", 128), ("e2a", 256), ("w1", 512),
                  ("e3b", 256), ("e2b", 512), ("e2c", 512), ("e1a", 256), ("e1b", 256),
                  ("w2", 512), ("e0d", 2 * OC), ("e1d", 2 * OC), ("e2d", 2 * OC), ("e3d", 2 * OC)):
    W_COLS[_name] = (_at, _at + _n)
    _at += _n
W_TOTAL = _at
W_HEAD = W_COLS["zdt"][1]

V_LN1W, V_LN1B, V_N1W, V_LN2W, V_LN2B, V_N2W = range(6)
V_B1, V_NORM, V_CONVB, V_CONVW, V_DCH = 6, 10, 12, 15, 27
V_TOTAL = 29
R_DTB, R_ALOG, R_QN, R_KN, R_B2 = 0, 4, 8, 16, 24
R_TOTAL = 24 + D


def build(nc, x, weights, vectors, rows, consts, out):
    with ExitStack() as ctx:
        def sb(name, shape, dt=F32):
            return ctx.enter_context(nc.sbuf_tensor("sb_" + name, shape, dt))

        def ps(name, shape, dt=F32):
            return ctx.enter_context(nc.psum_tensor(name, shape, dt))

        per, lead, made = {}, {}, []

        def signal(name, per_round, ahead=0):
            sem = ctx.enter_context(nc.semaphore(name))
            per[sem.name], lead[sem.name] = per_round, ahead
            made.append(sem)
            return sem

        def at(sem, r, k):
            return (r + 2 + lead[sem.name]) * per[sem.name] + k

        W = sb("W", [P, W_TOTAL])
        vec = sb("vec", [P, V_TOTAL])
        row = sb("row", [P, R_TOTAL])
        cst = sb("cst", [P, 5 * P + 16])
        ident = cst[:, 0:P]
        upto = cst[:, P:2 * P]
        after = cst[:, 2 * P:3 * P]
        ones = cst[:, 3 * P:4 * P]
        future = cst[:, 4 * P:5 * P]
        before = cst[:, 5 * P:5 * P + 16].rearrange("p (e f) -> p e f", e=E)
        identb = sb("identb", [P, P], BF16)
        maskb = sb("maskb", [P, P], BF16)
        minus_half = sb("minus_half", [P, 8])
        eps = sb("eps", [P, 2])
        wqk = sb("wqk", [P, 2, AH, HD])
        neg_a = sb("neg_a", [P, NH])
        diag_d = sb("diag_d", [P, 2, P])

        def w(name):
            a, b = W_COLS[name]
            return W[:, a:b]

        def w2(name, n):
            return w(name).rearrange("p (h n) -> p h n", n=n)

        xin = sb("xin", [P, T, D])
        xres = sb("xres", [P, T, D])
        xn = sb("xn", [P, T, D])
        xa = sb("xa", [P, T, D])
        xb = sb("xb", [P, T, D])
        xaT = sb("xaT", [P, L])
        xbT = sb("xbT", [P, L])
        st6 = sb("st6", [P, T, 6])
        mv = sb("mv", [P, T, 2])
        lnv = sb("lnv", [P, 8, T])
        qk = sb("qk", [P, T, 2, AH, HD])
        sq = sb("sq", [P, T, 2, AH, HD])
        rqk = sb("rqk", [P, 3, T * 2 * AH])
        tokqk = sb("tokqk", [P, T, 2, AH, 32])
        qT = sb("qT", [P, G, L], F32R)
        kT = sb("kT", [P, G, L], F32R)
        va = sb("va", [P, T, AH, 32])
        mx = sb("mx", [P, T, G, 4])
        mhl = sb("mhl", [P, G, T, 4, 2])
        mT = sb("mT", [8, 2, L], F32R)
        pr = sb("pr", [P, 4, 2, L])
        oT = sb("oT", [P, 2, L])
        rden = sb("rden", [P, T, 4])
        ao = sb("ao", [P, T, D])
        aoT = sb("aoT", [P, L])
        xc = sb("xc", [P, 3, L + 3])
        cv = sb("cv", [P, 3, L])
        cm = sb("cm", [P, L])
        xact = sb("xact", [P, 3, L])
        cT = sb("cT", [NS, L])
        zraw = sb("zraw", [P, T, DI + NH])
        zs = zraw[:, :, 0:DI]
        sp = sb("sp", [P, 10, T, NH])
        dt = sb("dt", [P, T, NH])
        dta = sb("dta", [P, T, NH])
        dec = sb("dec", [P, 3, T, NH])
        rs = sb("rs", [P, 2, NH, P])
        es = sb("es", [P, 2, NH, P])
        gm = sb("gm", [P, 2, P])
        wm = sb("wm", [P, 2, NH, P])
        xdt = sb("xdt", [P, 2, DI])
        xw = sb("xw", [P, 2, DI])
        btok = sb("btok", [P, 2, NS])
        hst = sb("hst", [NS, DI])
        hdec = sb("hdec", [NS, DI])
        yc = sb("yc", [P, 2, DI])
        yz = sb("yz", [P, 2, DI])
        junk = sb("junk", [P, 2, DI])
        yss = sb("yss", [P, T])
        ry = sb("ry", [P, 3, T])
        yT = sb("yT", [P, 2, L])
        x1 = sb("x1", [P, T, D])
        x1n = sb("x1n", [P, T, D])
        x1T = sb("x1T", [P, L])
        st2 = sb("st2", [P, T, 6])
        mv2 = sb("mv2", [P, T, 2])
        r2 = sb("r2", [P, 2, T])
        x2 = sb("x2", [P, T, D])
        x2ss = sb("x2ss", [P, T])
        r3 = sb("r3", [P, 3, T])
        xf = sb("xf", [P, T, D])
        xfT = sb("xfT", [P, L])
        gt = sb("gt", [P, 12, T, E])
        g1 = sb("g1", [P, 4, T])
        gq = sb("gq", [P, 2, T, E, E])
        wts = sb("wts", [P, T, E])
        share = pr[:].rearrange("p a h l -> p (a h) l")
        hm, h0, h2c = share[:, 0:4], share[:, 4:6], share[:, 6:8]
        h2a = rs[:].rearrange("p k h t -> p k (h t)")
        h2b = es[:].rearrange("p k h t -> p k (h t)")
        h1a = wm[:].rearrange("p k h t -> p k (h t)")
        h1 = sb("h1", [P, 2, L])
        h3a = sb("h3a", [P, L])
        h3b = sb("h3b", [P, 2, L])
        gs = sb("gs", [P, T, D])

        S = [ps(f"S{i}", [P, 2, L]) for i in range(2)]
        R = [ps(f"R{i}", [P, L]) for i in range(4)]

        S_flat = [p[:].rearrange("p b n -> p (b n)") for p in S]
        pr_flat = [pr[:, i].rearrange("p b n -> p (b n)") for i in range(4)]

        def bank(i):
            return S[i // 2][:, i % 2, :]

        c_loaded = signal("c_loaded", 0)
        wh_loaded = signal("wh_loaded", 0)
        wt_loaded = signal("wt_loaded", 0)
        x_loaded = signal("x_loaded", 16, 1)
        xres_loaded = signal("xres_loaded", 16)
        c_moved = signal("c_moved", 16)
        m_moved = [signal(f"m_moved{g}", 4 * 16) for g in range(G)]
        out_stored = signal("out_stored", 16)

        last_silu = signal("last_silu", 0)
        last_join = signal("last_join", 0)
        last_stored = signal("last_stored", 0)

        pool_set = signal("pool_set", 0)
        dve_set = signal("dve_set", 0)
        act_set = signal("act_set", 0)

        pool_passed = signal("pool_passed", 0)
        dve_passed = signal("dve_passed", 0)

        made.clear()
        qkv_ps = signal("qkv_ps", T)
        xbc_ps = signal("xbc_ps", 3)
        z_ps = signal("z_ps", T)
        op_ps = signal("op_ps", 1)
        ot_ps = signal("ot_ps", G - 1)
        ot3_ps = signal("ot3_ps", 1)
        aoT_ps = signal("aoT_ps", 1)
        wo_ps = signal("wo_ps", 1)
        xfT_ps = signal("xfT_ps", 1)
        x1T_ps = signal("x1T_ps", 1)
        gate_ps = signal("gate_ps", 1)
        up_ps = signal("up_ps", 19)
        qkT_ps = signal("qkT_ps", 2 * G)
        s_ps = signal("s_ps", G * UNITS)
        mT_ps = signal("mT_ps", G)
        e_ps = signal("e_ps", G * UNITS)
        pv_ps = signal("pv_ps", G * UNITS)
        s_half_ps = signal("s_half_ps", 2 * G)
        e_half_ps = signal("e_half_ps", 2 * G)
        cum_ps = signal("cum_ps", 1)
        seg_ps = signal("seg_ps", T)
        xt_ps = signal("xt_ps", T)
        y_ps = signal("y_ps", T)
        hn_ps = signal("hn_ps", T - 1)
        yT_ps = signal("yT_ps", T)
        mlp_ps = signal("mlp_ps", 1)
        moe_ps = signal("moe_ps", T)
        xaT_ps = signal("xaT_ps", 1, 1)
        xbT_ps = signal("xbT_ps", 1, 1)

        pe_sems = made[:]
        made.clear()
        ry_sb = signal("ry_sb", 2)
        r2_sb = signal("r2_sb", 2)
        r3_sb = signal("r3_sb", 2)
        qkv_sb = signal("qkv_sb", T)
        sq_sb = signal("sq_sb", 1)
        xc_sb = signal("xc_sb", 3)
        rqk_sb = signal("rqk_sb", 2)
        z_sb = signal("z_sb", T)
        aoT_sb = signal("aoT_sb", 1)
        x2ss_sb = signal("x2ss_sb", 1)
        xfT_sb = signal("xfT_sb", 1)
        x1T_sb = signal("x1T_sb", 1)
        gexp_sb = signal("gexp_sb", 1)
        spe_sb = signal("spe_sb", 1)
        qT_sb = signal("qT_sb", G)
        mT_sb = signal("mT_sb", G)
        act_up = signal("act_up", 17)
        conv_act = signal("conv_act", 2)
        conv_sb = signal("conv_sb", 1)
        zs_sb = signal("zs_sb", 1)
        dec_sb = signal("dec_sb", 1)
        seg_sb = signal("seg_sb", T)
        p_sb = signal("p_sb", G * UNITS)
        oT_sb = signal("oT_sb", G)
        yss_sb = signal("yss_sb", T)
        yT_sb = signal("yT_sb", T)
        xaT_sb = signal("xaT_sb", 1, 1)
        xbT_sb = signal("xbT_sb", 1, 1)
        gs_sb = signal("gs_sb", 1)

        act_sems = made[:]
        made.clear()
        ao_sb = signal("ao_sb", 2 * (G - 1))
        ao3_sb = signal("ao3_sb", 2)
        x1_sb = signal("x1_sb", T)
        ssqk_sb = signal("ssqk_sb", 1)
        ln2_sb = signal("ln2_sb", 2)
        x2_sb = signal("x2_sb", 2)
        nqk_sb = signal("nqk_sb", 4)
        lo_sb = signal("lo_sb", 1)
        xf_sb = signal("xf_sb", 1)
        x1n_sb = signal("x1n_sb", 1)
        gate_sb = signal("gate_sb", 6)
        wts_sb = signal("wts_sb", 13)
        spa_sb = signal("spa_sb", 2)
        dt_sb = signal("dt_sb", 15)
        kT_sb = signal("kT_sb", G)
        conv_dve = signal("conv_dve", 2 * (TAPS - 1))
        mx_sb = signal("mx_sb", G * UNITS)
        mhl_sb = signal("mhl_sb", 2 * G)
        h1_sb = signal("h1_sb", 2)
        sv_sb = signal("sv_sb", 1)
        moe_sb = signal("moe_sb", T * E)
        gr_sb = signal("gr_sb", 1 + T)
        og_sb = signal("og_sb", 3)
        xn_sb = signal("xn_sb", 1)
        xdt_sb = signal("xdt_sb", T)
        gm_sb = signal("gm_sb", T)
        wm_sb = signal("wm_sb", T)
        yc_sb = signal("yc_sb", 2 * (T - 1))
        yz_sb = signal("yz_sb", T)
        h_sb = signal("h_sb", 1 + 2 * (T - 2))
        stat_sb = signal("stat_sb", 2, 1)
        xab_sb = signal("xab_sb", 1, 1)

        dve_sems = made[:]
        made.clear()
        x1b_sb = signal("x1b_sb", 1)
        conv_pool = signal("conv_pool", 2 * TAPS - 1)
        rs_sb = signal("rs_sb", T)
        pm_sb = signal("pm_sb", G * UNITS)
        xw_sb = signal("xw_sb", T - 1)
        rn_sb = signal("rn_sb", 8, 1)

        pool_sems = made[:]

        block = ctx.enter_context(nc.Block())

        def score_pair(e):
            return e % 2 if e > LAST_MAX + 2 else 1

        def blocks(flat, u, n=None):
            cols, stride, heads = UNIT[u]
            return flat.rearrange("p (h n) -> p h n", n=stride)[:, 0:len(heads), 0:n or cols]

        @block.sync
        def _(sp_e):
            for sem in (x_loaded, xres_loaded, c_moved, *m_moved, out_stored):
                sp_e.sem_inc(sem, per[sem.name])
            sp_e.dma_start(xin[:], x[0].rearrange("(t p) c -> p t c", p=P)).then_inc(x_loaded, 16)
            sp_e.dma_start(cst[:], consts).then_inc(c_loaded, 16)
            sp_e.dma_start(vec[:], vectors).then_inc(c_loaded, 16)
            sp_e.dma_start(row[:], rows).then_inc(c_loaded, 16)
            sp_e.dma_start(W[:, 0:W_HEAD], weights[:, 0:W_HEAD]).then_inc(wh_loaded, 16)
            sp_e.dma_start(W[:, W_HEAD:W_TOTAL], weights[:, W_HEAD:W_TOTAL]).then_inc(wt_loaded, 16)
            sp_e.sem_inc(xres_loaded, 16)
            sp_e.sem_inc(out_stored, 16)

            def move_maxima(r, g):
                sp_e.wait_ge(mT_sb, at(mT_sb, r, g + 1))
                for j in range(4):
                    sp_e.dma_start(qT[32 * j + 24:32 * j + 26, g, :].bitcast(F32),
                                   mT[2 * j:2 * j + 2, g % 2, :].bitcast(F32))\
                        .then_inc(m_moved[g], 16)

            def rnd(r, tail, head, nxt):
                if tail:
                    sp_e.wait_ge(out_stored, at(out_stored, r, 0))
                    sp_e.dma_start(xres[:], x[r].rearrange("(t p) c -> p t c", p=P))\
                        .then_inc(xres_loaded, 16)
                if head:
                    move_maxima(r, 0)
                    move_maxima(r, 1)
                    sp_e.wait_ge(conv_sb, at(conv_sb, r, 1))
                    sp_e.wait_ge(y_ps, at(y_ps, r, 0))
                    sp_e.dma_start(cT[:], xact[NS:2 * NS, 2, :]).then_inc(c_moved, 16)
                    sp_e.wait_ge(xn_sb, at(xn_sb, r, 1))
                    sp_e.wait_ge(xab_sb, at(xab_sb, r, 0))
                    sp_e.dma_start(xin[:], x[nxt].rearrange("(t p) c -> p t c", p=P))\
                        .then_inc(x_loaded, 16)
                    move_maxima(r, 2)
                    move_maxima(r, 3)
                if tail and head:
                    sp_e.wait_ge(og_sb, at(og_sb, r, 3))
                    sp_e.dma_start(out[r].rearrange("(t p) c -> p t c", p=P), xres[:])\
                        .then_inc(out_stored, 16)

            rnd(-1, False, True, 1)
            with sp_e.Fori(0, B - 2) as r:
                rnd(r, True, True, r + 2)
            rnd(B - 2, True, True, B - 1)
            rnd(B - 1, True, False, None)
            for t in range(T):
                sp_e.wait_ge(last_join, 2 * t + 2)
                sp_e.dma_start(out[B - 1, t * P:(t + 1) * P, :], xres[:, t, :]).then_inc(last_stored, 16)
            sp_e.wait_ge(out_stored, at(out_stored, B - 1, 0))
            sp_e.wait_ge(last_stored, 16 * T)

        @block.tensor
        def _(pe):
            def mm(o, lhsT, rhs, start=True, stop=True):
                return pe.matmul(o, lhsT, rhs, start=start, stop=stop, skip_group_check=True)

            def transposes(o, src):
                for t in range(T):
                    i = pe.transpose(o[:, t * P:(t + 1) * P], src(t), ident)
                return i

            def prep_a(r):
                pe.wait_ge(xab_sb, at(xab_sb, r, 1))
                pe.wait_ge(seg_sb, at(seg_sb, r, T))
                transposes(R[1], lambda t: xa[:, t, :]).then_inc(xaT_ps, 1)

            def prep_b(r):
                pe.wait_ge(xaT_sb, at(xaT_sb, r, 1))
                transposes(R[1], lambda t: xb[:, t, :]).then_inc(xbT_ps, 1)

            def max_scores(r, m, halves=(0, 1)):
                g, u = m // UNITS, m % UNITS
                n, stride, heads = UNIT[u]
                i = n // P - 1
                pair = m % 2 if g < 2 else 0
                per_bank = L // stride
                if 0 not in halves:
                    pass
                elif m < 2:
                    pe.wait_ge(qT_sb, at(qT_sb, r, G))
                    pe.wait_ge(kT_sb, at(kT_sb, r, G))
                elif g < 2:
                    pe.wait_ge(mx_sb, at(mx_sb, r, m - 1))
                elif m == 2 * UNITS:
                    pe.wait_ge(dec_sb, at(dec_sb, r, 1))
                else:
                    pe.wait_ge(mx_sb, at(mx_sb, r, m))
                out = S[pair][:].rearrange("p b (h n) -> p b h n", n=stride)
                for b in range(2 if 0 in halves else 0):
                    mm(out[:, b, :, i * P:(i + 1) * P], identb[:],
                       maskb[:].unsqueeze(1).broadcast_to([P, per_bank, P]), True, False)
                for h in range(per_bank):
                    if h not in halves:
                        continue
                    if h:
                        pe.wait_ge(s_half_ps, at(s_half_ps, r, 2 * g + u - 3))
                    for b in range(2):
                        j = 32 * heads[b * per_bank + h]
                        o = mm(out[:, b, h, 0:n], qT[j:j + 32, g, i * P:(i + 1) * P], kT[j:j + 32, g, 0:n],
                               False, True)
                    o.then_inc(s_half_ps if h < per_bank - 1 else s_ps, 1)

            def turn_maxima(r, g, o):
                pe.wait_ge(mhl_sb, at(mhl_sb, r, 2 * g + 2))
                if g >= 2:
                    pe.wait_ge(seg_sb, at(seg_sb, r, g))
                for t in range(T):
                    i = pe.transpose(o[0:8, t * P:(t + 1) * P],
                                     mhl[:, g, t].rearrange("p j x -> p (j x)"), ident)
                i.then_inc(mT_ps, 1)

            def exp_scores(r, e, halves=(0, 1)):
                g, u = e // UNITS, e % UNITS
                n, stride, heads = UNIT[u]
                if 0 not in halves:
                    pass
                elif e == 0:
                    pe.wait_ge(mx_sb, at(mx_sb, r, 2 * UNITS))
                elif score_pair(e) == 1 == score_pair(e - 1):
                    pe.wait_ge(p_sb, at(p_sb, r, e))
                elif score_pair(e - 2) == 1 and score_pair(e) == 0:
                    pe.wait_ge(mx_sb, at(mx_sb, r, 4 * UNITS))
                else:
                    pe.wait_ge(p_sb, at(p_sb, r, e - 1))
                if u == 0:
                    pe.wait_ge(m_moved[g], at(m_moved[g], r, 64))
                per_bank = L // stride
                out = S[score_pair(e)][:].rearrange("p b (h n) -> p b h n", n=stride)
                for h in range(per_bank):
                    if h not in halves:
                        continue
                    if h:
                        pe.wait_ge(e_half_ps, at(e_half_ps, r, 2 * g + u - 3))
                    for b in range(2):
                        j = 32 * heads[b * per_bank + h]
                        o = mm(out[:, b, h, 0:n], kT[j:j + 32, g, L - n:L - n + P], qT[j:j + 32, g, L - n:L])
                    o.then_inc(e_half_ps if h < per_bank - 1 else e_ps, 1)

            def weigh_values(r, e):
                g, u = e // UNITS, e % UNITS
                n, stride, heads = UNIT[u]
                i = T - n // P
                pe.wait_ge(pm_sb, at(pm_sb, r, e + 1))
                pe.wait_ge(p_sb, at(p_sb, r, e + 1))
                if u == 0:
                    if g == 0:
                        pe.wait_ge(moe_sb, at(moe_sb, r, 3 * E))
                    else:
                        pe.wait_ge(oT_sb, at(oT_sb, r, g))
                p = blocks(pr_flat[e % 4], u)
                for h, j in enumerate(heads):
                    o = mm(R[0][32 * j:32 * j + 32, i * P:L], va[:, i, 4 * g + j, :], p[:, h, :],
                           i == 0, i == T - 1)
                o.then_inc(pv_ps, 1)

            def turn_values(r, g):
                pe.wait_ge(oT_sb, at(oT_sb, r, g + 1))
                pe.wait_ge(yz_sb, at(yz_sb, r, g + 1))
                for t in range(T):
                    i = pe.transpose(R[3][:, t * P:(t + 1) * P], oT[:, g % 2, t * P:(t + 1) * P], ident)
                i.then_inc(ot_ps, 1)

            def cumulate(r):
                pe.wait_ge(dt_sb, at(dt_sb, r, 15))
                pe.wait_ge(mx_sb, at(mx_sb, r, 2 * UNITS - 1))
                flat = dta[:].rearrange("p c h -> p (c h)")
                for n, lhs in enumerate((upto, after, ones)):
                    i = mm(S[0][:, 0, 16 * n:16 * n + 16], lhs, flat)
                i.then_inc(cum_ps, 1)

            def segments(r, c):
                pe.wait_ge(rs_sb, at(rs_sb, r, c + 1))
                if c == 0:
                    pe.wait_ge(moe_sb, at(moe_sb, r, 4 * E))
                elif c == 1:
                    pe.wait_ge(h_sb, at(h_sb, r, 1))
                else:
                    pe.wait_ge(h_sb, at(h_sb, r, 2 * c - 1))
                mm(R[1][:, :], after, rs[:, c % 2].rearrange("p h t -> p (h t)")).then_inc(seg_ps, 1)

            def scan_inputs(r, c):
                s = slice(c * P, (c + 1) * P)
                pe.wait_ge(conv_sb, at(conv_sb, r, 1))
                pe.wait_ge(c_moved, at(c_moved, r, 16))
                if c == 0:
                    pe.wait_ge(moe_sb, at(moe_sb, r, E))
                else:
                    pe.wait_ge(yT_sb, at(yT_sb, r, c))
                for n in range(3):
                    pe.transpose(R[2][:, n * P:(n + 1) * P], xact[:, n, s], ident)
                mm(R[2][:, 3 * P:4 * P], xact[0:NS, 2, s], cT[:, s]).then_inc(xt_ps, 1)

            def scan_outputs(r, c):
                s = slice(c * P, (c + 1) * P)
                pe.wait_ge(wm_sb, at(wm_sb, r, c + 1))
                pe.wait_ge(xdt_sb, at(xdt_sb, r, c + 1))
                if c == 0:
                    pe.wait_ge(moe_sb, at(moe_sb, r, 2 * E))
                else:
                    pe.wait_ge(h_sb, at(h_sb, r, 2 * c - 1))
                    pe.wait_ge(ao_sb, at(ao_sb, r, 2 * c))
                    mm(R[3][:, DI:2 * DI], cT[:, s], hst[:], True, False)
                for n in range(2):
                    mm(R[3][:, n * P:(n + 1) * P], xact[:, n, s], diag_d[:, n, :], c == 0 and n == 0, False)
                for h in range(NH):
                    i = mm(R[3][:, h * HP:(h + 1) * HP], wm[:, c % 2, h, :],
                           xdt[:, c % 2, h * HP:(h + 1) * HP], False, True)
                i.then_inc(y_ps, 1)

            def new_state(r, c):
                pe.wait_ge(xw_sb, at(xw_sb, r, c + 1))
                pe.wait_ge(gm_sb, at(gm_sb, r, c + 1))
                pe.wait_ge(seg_sb, at(seg_sb, r, c + 1))
                if c >= 1:
                    pe.wait_ge(mT_sb, at(mT_sb, r, c + 2))
                mm(R[1][0:NS, 0:DI], btok[:, c % 2, :], xw[:, c % 2, :]).then_inc(hn_ps, 1)

            def turn_y(r, c):
                pe.wait_ge(yz_sb, at(yz_sb, r, c + 1))
                pe.wait_ge(gm_sb, at(gm_sb, r, c + 1))
                for n in range(2):
                    i = pe.transpose(R[2][:, n * P:(n + 1) * P], yz[:, c % 2, n * P:(n + 1) * P], ident)
                i.then_inc(yT_ps, 1)

            def ring_free(r, k):
                if k == 0:
                    pe.wait_ge(xfT_sb, at(xfT_sb, r, 1))
                elif k == 1:
                    pe.wait_ge(x1T_sb, at(x1T_sb, r, 1))
                elif k == 2:
                    pe.wait_ge(gate_sb, at(gate_sb, r, 1))
                elif k == 3:
                    pe.wait_ge(x2_sb, at(x2_sb, r, 2))
                elif k - 4 <= 14:
                    pe.wait_ge(act_up, at(act_up, r, k - 3))
                elif k - 4 == 15:
                    pe.wait_ge(mT_sb, at(mT_sb, r, 1))
                elif k - 4 in (16, 17):
                    pe.wait_ge(act_up, at(act_up, r, k - 4))
                elif k - 4 in (18, 19):
                    pe.wait_ge(h1_sb, at(h1_sb, r, k - 21))
                elif k - 4 == 20:
                    pe.wait_ge(sv_sb, at(sv_sb, r, 1))
                else:
                    pe.wait_ge(mT_sb, at(mT_sb, r, 2))

            def up(r, k, name, n, src, ins=None):
                ring_free(r, k)
                if ins is not None:
                    pe.wait_ge(act_up, at(act_up, r, ins))
                if len(src) == 1:
                    lhs = [w(name)[:, n * P:(n + 1) * P]]
                else:
                    lhs = [w2(name, 256)[:, kk, n * P:(n + 1) * P] for kk in range(2)]
                for kk, (a, b) in enumerate(zip(lhs, src)):
                    i = mm(R[k % 4][:, :], a, b, kk == 0, kk == len(src) - 1)
                i.then_inc(up_ps, 1)

            def experts_down(r, t, head):
                if t == 3 and not head:
                    pe.wait_ge(act_up, at(act_up, r, 17))
                else:
                    ring_free(r, 22 + t)
                if t == 0:
                    pe.wait_ge(act_up, at(act_up, r, 17))
                    pe.wait_ge(h1_sb, at(h1_sb, r, 2))
                for e, (h, name) in enumerate(((h0, "e0d"), (h1, "e1d"), (h2c, "e2d"), (h3b, "e3d"))):
                    for n in range(2):
                        i = mm(R[(22 + t) % 4][:, e * OC:(e + 1) * OC], h[:, n, t * P:(t + 1) * P],
                               w2(name, OC)[:, n, :], n == 0, n == 1)
                i.then_inc(moe_ps, 1)

            def project_x(r, n):
                pe.wait_ge(qkv_sb, at(qkv_sb, r, n + 1))
                mm(bank(n), w("x")[:, n * P:(n + 1) * P], xaT[:]).then_inc(xbc_ps, 1)

            def project_z(r, n):
                t = (3, 0, 1, 2)[n]
                if n == 0:
                    pe.wait_ge(qkv_sb, at(qkv_sb, r, T))
                else:
                    pe.wait_ge(xc_sb, at(xc_sb, r, n))
                mm(bank(t)[:, 0:DI + NH], xaT[:, t * P:(t + 1) * P], w("zdt")).then_inc(z_ps, 1)

            def stage_b(r, tail, head):
                if tail:
                    pe.wait_ge(yT_sb, at(yT_sb, r, 0))
                    for t in range(T):
                        for n in range(2):
                            i = mm(R[2][:, t * P:(t + 1) * P], yT[:, n, t * P:(t + 1) * P],
                                   w2("op", D)[:, n, :], n == 0, n == 1)
                    i.then_inc(op_ps, 1)
                    pe.wait_ge(oT_sb, at(oT_sb, r, 0))
                    pe.wait_ge(yz_sb, at(yz_sb, r, 0))
                    for t in range(T):
                        i = pe.transpose(R[3][:, t * P:(t + 1) * P], oT[:, 1, t * P:(t + 1) * P], ident)
                    i.then_inc(ot3_ps, 1)
                if head:
                    pe.wait_ge(xbT_sb, at(xbT_sb, r, 0))
                    pe.wait_ge(p_sb, at(p_sb, r, 0))
                    for t in range(T):
                        mm(bank(t)[:, 0:3 * D], xbT[:, t * P:(t + 1) * P], w("qkv")).then_inc(qkv_ps, 1)
                if tail:
                    pe.wait_ge(ao3_sb, at(ao3_sb, r, 2))
                    transposes(R[0], lambda t: ao[:, t, :]).then_inc(aoT_ps, 1)
                if head:
                    project_x(r, 0)
                if tail:
                    pe.wait_ge(aoT_sb, at(aoT_sb, r, 1))
                    for t in range(T):
                        i = mm(R[3][:, t * OC:(t + 1) * OC], aoT[:, t * P:(t + 1) * P], w("wo"))
                    i.then_inc(wo_ps, 1)
                if head:
                    project_x(r, 1)
                    project_x(r, 2)
                    project_z(r, 0)
                    project_z(r, 1)
                if tail:
                    pe.wait_ge(x1n_sb, at(x1n_sb, r, 1))
                    pe.wait_ge(xbT_sb, at(xbT_sb, r, 0))
                    transposes(R[1], lambda t: x1n[:, t, :]).then_inc(x1T_ps, 1)
                    pe.wait_ge(xf_sb, at(xf_sb, r, 1))
                    transposes(R[0], lambda t: xf[:, t, :]).then_inc(xfT_ps, 1)
                if head:
                    project_z(r, 2)
                    project_z(r, 3)
                if tail:
                    pe.wait_ge(xfT_sb, at(xfT_sb, r, 1))
                    pe.wait_ge(x1_sb, at(x1_sb, r, T))
                    for t in range(T):
                        i = mm(R[2][:, t * E:(t + 1) * E], xfT[:, t * P:(t + 1) * P], w("gate"))
                    i.then_inc(gate_ps, 1)
                    up(r, 0, "e0u", 0, [xfT[:]])
                    up(r, 1, "e0u", 1, [xfT[:]])
                    up(r, 2, "e3a", 0, [xfT[:]])
                if head:
                    for n in range(2 * G):
                        if n == 0:
                            pe.wait_ge(lo_sb, at(lo_sb, r, 1))
                        if n < T:
                            pe.wait_ge(z_sb, at(z_sb, r, (2, 3, 4, 1)[n]))
                        elif n % 2 == 0:
                            pe.wait_ge(qT_sb, at(qT_sb, r, (n - 4) // 2 + 1))
                        else:
                            pe.wait_ge(kT_sb, at(kT_sb, r, (n - 4) // 2 + 1))
                        transposes(bank(n % 4),
                                   lambda t: tokqk[:, t, n % 2, 4 * (n // 2):4 * (n // 2) + 4, :]
                                   .rearrange("p j x -> p (j x)")).then_inc(qkT_ps, 1)

                def m_unit(m, halves=(0, 1)):
                    if head:
                        max_scores(r, m, halves)

                x_in = [xfT[:]]
                if tail:
                    up(r, 3, "e2a", 0, x_in)
                m_unit(0)
                if tail:
                    up(r, 4, "e2a", 1, x_in)
                m_unit(1)
                if tail:
                    up(r, 5, "w1", 0, [x1T[:]])
                m_unit(2)
                if tail:
                    up(r, 6, "w1", 1, [x1T[:]])
                m_unit(3)
                if tail:
                    up(r, 7, "e3b", 0, [h3a[:]], 3)
                m_unit(4, (0,))
                if tail:
                    up(r, 8, "e3b", 1, [h3a[:]])
                m_unit(4, (1,))
                m_unit(5, (0,))
                if tail:
                    up(r, 9, "e2b", 0, [h2a[:, 0], h2a[:, 1]], 5)
                m_unit(5, (1,))
                m_unit(6)
                if tail:
                    up(r, 10, "e2b", 1, [h2a[:, 0], h2a[:, 1]])
                m_unit(7)
                if tail:
                    up(r, 11, "w1", 2, [x1T[:]])
                m_unit(8)
                if tail:
                    up(r, 12, "w1", 3, [x1T[:]])
                m_unit(9)
                if tail:
                    up(r, 13, "e2c", 0, [h2b[:, 0], h2b[:, 1]], 11)
                if tail:
                    up(r, 14, "e2c", 1, [h2b[:, 0], h2b[:, 1]])
                if head:
                    ring_free(r, 15)
                    turn_maxima(r, 0, R[3])
                if tail:
                    up(r, 16, "e1a", 0, x_in)
                m_unit(10, (0,))
                if tail:
                    up(r, 17, "e1a", 1, x_in)
                m_unit(10, (1,))
                m_unit(11, (0,))
                if tail:
                    up(r, 18, "e1b", 0, x_in)
                m_unit(11, (1,))
                if tail:
                    if head:
                        ring_free(r, 19)
                    else:
                        pe.wait_ge(act_up, at(act_up, r, 12))
                    mm(R[19 % 4][:, :], w("e1b")[:, P:2 * P], xfT[:]).then_inc(up_ps, 1)
                if tail:
                    ring_free(r, 20)
                    pe.wait_ge(act_up, at(act_up, r, 13))
                    for t in range(T):
                        for n in range(4):
                            i = mm(R[0][:, t * P:(t + 1) * P], hm[:, n, t * P:(t + 1) * P],
                                   w("w2")[:, n * D:(n + 1) * D], n == 0, n == 3)
                    i.then_inc(mlp_ps, 1)
                if head:
                    ring_free(r, 21)
                    turn_maxima(r, 1, R[1])
                    cumulate(r)

                if tail:
                    experts_down(r, 0, head)
                if head:
                    exp_scores(r, 0)
                    max_scores(r, MAX_AT[0])
                if tail:
                    experts_down(r, 1, head)
                if head:
                    exp_scores(r, 1)
                    max_scores(r, MAX_AT[1])
                if tail:
                    experts_down(r, 2, head)
                    experts_down(r, 3, head)

            def stage_a(r):
                scan_inputs(r, 0)
                for e in range(G * UNITS):
                    g, u = e // UNITS, e % UNITS
                    if e > 1:
                        exp_scores(r, e, (0,))
                    if e > 1 and e in MAX_AT:
                        max_scores(r, MAX_AT[e], (0,))
                    if u == 4:
                        if e not in MAX_AT:
                            weigh_values(r, e - 2)
                        exp_scores(r, e, (1,))
                        if e in MAX_AT and MAX_AT[e] % UNITS > 3:
                            max_scores(r, MAX_AT[e], (1,))
                        scan_outputs(r, g)
                    if u == 5:
                        if g < T - 1:
                            new_state(r, g)
                        else:
                            prep_b(r)
                        exp_scores(r, e, (1,))
                        if e in MAX_AT and MAX_AT[e] % UNITS > 3:
                            max_scores(r, MAX_AT[e], (1,))
                    if u == 0 and g > 0:
                        turn_y(r, g - 1)
                    if e == 2:
                        segments(r, 0)
                    if e > 1 and not (u == 4 and e not in MAX_AT):
                        weigh_values(r, e - 2)
                    if u < 4 and e > 1 and e in MAX_AT and MAX_AT[e] % UNITS > 3:
                        max_scores(r, MAX_AT[e], (1,))
                    if u == 1 and g > 0:
                        segments(r, g)
                        scan_inputs(r, g)
                    if u == 3 and g >= 1:
                        turn_values(r, g - 1)
                    if (g, u) in ((1, 2), (2, 3)):
                        turn_maxima(r, g + 1, R[1])
                    if (g, u) == (3, 3):
                        prep_a(r)
                turn_y(r, T - 1)
                for e in (G * UNITS - 2, G * UNITS - 1):
                    weigh_values(r, e)

            for sem in pe_sems:
                pe.sem_inc(sem, per[sem.name])
            for sem in (op_ps, ot3_ps, aoT_ps, wo_ps, xfT_ps, x1T_ps, gate_ps, up_ps, mlp_ps, moe_ps):
                pe.sem_inc(sem, per[sem.name])
            pe.wait_ge(c_loaded, 48)
            pe.wait_ge(pool_set, 8)
            pe.wait_ge(dve_set, 7)
            pe.wait_ge(xab_sb, at(xab_sb, -2, 1))
            transposes(R[1], lambda t: xa[:, t, :]).then_inc(xaT_ps, 1)
            pe.wait_ge(xaT_sb, at(xaT_sb, -2, 1))
            transposes(R[1], lambda t: xb[:, t, :]).then_inc(xbT_ps, 1)
            pe.wait_ge(wh_loaded, 16)
            stage_b(-1, False, True)
            stage_a(-1)
            pe.wait_ge(wt_loaded, 16)
            with pe.Fori(0, B - 1) as r:
                stage_b(r, True, True)
                stage_a(r)
            stage_b(B - 1, True, False)

        @block.scalar
        def _(act):
            def evac_qkv(r):
                act.wait_ge(lo_sb, at(lo_sb, r, 0))
                act.wait_ge(pv_ps, at(pv_ps, r, 0))
                for t in range(T):
                    act.wait_ge(qkv_ps, at(qkv_ps, r, t + 1))
                    act.activation(qk[:, t].rearrange("p a h d -> p (a h d)"), bank(t)[:, 0:2 * D], ACT.Copy)
                    act.activation(va[:, t, :, 0:HD],
                                   bank(t)[:, 2 * D:3 * D].rearrange("p (h d) -> p h d", h=AH),
                                   ACT.Copy).then_inc(qkv_sb, 1)

            def evac_maxima(r, g, o):
                act.wait_ge(mT_ps, at(mT_ps, r, g + 1))
                if g < 2:
                    act.wait_ge(m_moved[g + 2], at(m_moved[g + 2], r, 0))
                else:
                    act.wait_ge(m_moved[g - 2], at(m_moved[g - 2], r, 64))
                act.activation(mT[:, g % 2, :], o[0:8, :], ACT.Copy).then_inc(mT_sb, 1)

            def evac_values(r, g):
                act.wait_ge(pv_ps, at(pv_ps, r, UNITS * (g + 1)))
                if g == 1:
                    act.wait_ge(ot3_ps, at(ot3_ps, r, 1))
                else:
                    act.wait_ge(ot_ps, at(ot_ps, r, g - 1 if g else 0))
                act.activation(oT[:, g % 2, :], R[0][:, :], ACT.Copy).then_inc(oT_sb, 1)

            def evac_y(r, c):
                act.wait_ge(yT_ps, at(yT_ps, r, c + 1))
                act.wait_ge(op_ps, at(op_ps, r, 1))
                for n in range(2):
                    i = act.activation(yT[:, n, c * P:(c + 1) * P], R[2][:, n * P:(n + 1) * P], ACT.Copy,
                                       scale=vec[:, V_NORM + n:V_NORM + n + 1])
                i.then_inc(yT_sb, 1)

            def evac_a(r):
                act.wait_ge(xaT_ps, at(xaT_ps, r, 1))
                act.wait_ge(z_ps, at(z_ps, r, T))
                act.activation(xaT[:], R[1][:, :], ACT.Identity, bias=vec[:, V_LN1B:V_LN1B + 1],
                               scale=vec[:, V_LN1W:V_LN1W + 1]).then_inc(xaT_sb, 1)

            def evac_b(r):
                act.wait_ge(xbT_ps, at(xbT_ps, r, 1))
                act.wait_ge(qkv_ps, at(qkv_ps, r, T))
                act.activation(xbT[:], R[1][:, :], ACT.Copy,
                               scale=vec[:, V_N1W:V_N1W + 1]).then_inc(xbT_sb, 1)

            def hidden(r, k, dst, func, bias=0.0):
                act.wait_ge(up_ps, at(up_ps, r, k + 1 if k < 15 else k))
                act.activation(dst, R[k % 4][:, :], func, bias=bias).then_inc(act_up, 1)

            def inverse_root(r, src, steps, sig, scale, which):
                act.activation(steps[:, 0, :], src, ACT.Ln, scale=scale,
                               bias=eps[:, which:which + 1]).then_inc(sig, 1)
                act.wait_ge(sig, at(sig, r, 1))
                act.activation(steps[:, 1, :], steps[:, 0, :], ACT.Exp, scale=-0.5).then_inc(sig, 1)

            def evac_xc(r, n):
                act.wait_ge(xbc_ps, at(xbc_ps, r, n + 1))
                act.activation(xc[:, n, 3:L + 3], bank(n), ACT.Copy).then_inc(xc_sb, 1)

            def evac_z(r, n):
                t = (3, 0, 1, 2)[n]
                act.wait_ge(z_ps, at(z_ps, r, n + 1))
                act.activation(zraw[:, t, :], bank(t)[:, 0:DI + NH], ACT.Copy).then_inc(z_sb, 1)

            def stage_b(r, tail, head):
                if tail:
                    act.wait_ge(yss_sb, at(yss_sb, r, 0))
                    act.wait_ge(x1_sb, at(x1_sb, r, 0))
                    inverse_root(r, yss[:], ry, ry_sb, 1.0 / DI, 0)
                if head:
                    evac_qkv(r)
                if tail:
                    act.wait_ge(aoT_ps, at(aoT_ps, r, 1))
                    act.activation(aoT[:], R[0][:, :], ACT.Copy).then_inc(aoT_sb, 1)
                if head:
                    act.wait_ge(qkv_sb, at(qkv_sb, r, T))
                    act.activation(sq[:], qk[:], ACT.Square).then_inc(sq_sb, 1)
                    act.wait_ge(conv_dve, at(conv_dve, r, 0))
                    act.wait_ge(conv_pool, at(conv_pool, r, 0))
                    evac_xc(r, 0)
                if tail:
                    act.wait_ge(ln2_sb, at(ln2_sb, r, 2))
                    act.wait_ge(x1n_sb, at(x1n_sb, r, 0))
                    inverse_root(r, mv2[:, :, 1], r2, r2_sb, 1.0, 0)
                    act.wait_ge(x2_sb, at(x2_sb, r, 2))
                    act.wait_ge(yss_sb, at(yss_sb, r, 0))
                    for t in range(T):
                        i = act.activation(junk[:, t // 2, t % 2 * D:t % 2 * D + D], x2[:, t, :], ACT.Square,
                                           accum_out=x2ss[:, t:t + 1])
                    i.then_inc(x2ss_sb, 1)
                    act.wait_ge(x2ss_sb, at(x2ss_sb, r, 1))
                    act.wait_ge(xf_sb, at(xf_sb, r, 0))
                    inverse_root(r, x2ss[:], r3, r3_sb, 1.0 / D, 1)
                if head:
                    evac_xc(r, 1)
                    act.wait_ge(ssqk_sb, at(ssqk_sb, r, 1))
                    act.activation(rqk[:, 1], rqk[:, 0], ACT.Ln, scale=1.0 / HD,
                                   bias=eps[:, 1:2]).then_inc(rqk_sb, 1)
                    evac_xc(r, 2)
                    act.wait_ge(rqk_sb, at(rqk_sb, r, 1))
                    act.activation(rqk[:, 2], rqk[:, 1], ACT.Exp, scale=-0.5).then_inc(rqk_sb, 1)
                    act.wait_ge(spa_sb, at(spa_sb, r, 0))
                    act.wait_ge(yz_sb, at(yz_sb, r, 0))
                    evac_z(r, 0)
                    evac_z(r, 1)
                if tail:
                    act.wait_ge(x1T_ps, at(x1T_ps, r, 1))
                    act.activation(x1T[:], R[1][:, :], ACT.Identity, bias=vec[:, V_LN2B:V_LN2B + 1],
                                   scale=vec[:, V_LN2W:V_LN2W + 1]).then_inc(x1T_sb, 1)
                    act.wait_ge(xfT_ps, at(xfT_ps, r, 1))
                    act.activation(xfT[:], R[0][:, :], ACT.Copy,
                                   scale=vec[:, V_N2W:V_N2W + 1]).then_inc(xfT_sb, 1)
                if head:
                    evac_z(r, 2)
                    evac_z(r, 3)
                    for n in range(2):
                        tap = V_CONVW + TAPS * n + TAPS - 1
                        act.wait_ge(xc_sb, at(xc_sb, r, n + 1))
                        act.wait_ge(conv_sb, at(conv_sb, r, 0))
                        act.activation(cv[:, n], xc[:, n, TAPS - 1:TAPS - 1 + L], ACT.Identity,
                                       bias=vec[:, V_CONVB + n:V_CONVB + n + 1],
                                       scale=vec[:, tap:tap + 1]).then_inc(conv_act, 1)
                    act.wait_ge(spa_sb, at(spa_sb, r, 2))
                    act.activation(sp[:, 2], sp[:, 1], ACT.Exp, scale=-1.0).then_inc(spe_sb, 1)
                if tail:
                    act.wait_ge(gate_sb, at(gate_sb, r, 6))
                    act.wait_ge(wts_sb, at(wts_sb, r, 0))
                    act.activation(gt[:, 5], gt[:, 4], ACT.Exp).then_inc(gexp_sb, 1)
                if head:
                    act.wait_ge(e_ps, at(e_ps, r, 0))
                    for g in range(G):
                        act.wait_ge(qkT_ps, at(qkT_ps, r, 2 * g + 1))
                        act.activation(qT[:, g, :], bank(2 * g % 4), ACT.Copy).then_inc(qT_sb, 1)
                if tail:
                    act.wait_ge(moe_ps, at(moe_ps, r, 0))
                    act.wait_ge(pv_ps, at(pv_ps, r, 0))
                    act.wait_ge(seg_ps, at(seg_ps, r, 0))
                    act.wait_ge(wm_sb, at(wm_sb, r, 0))
                    hidden(r, 0, h0[:, 0], ACT.Gelu)
                    hidden(r, 1, h0[:, 1], ACT.Gelu)
                    hidden(r, 2, h3a[:], ACT.Gelu)
                    hidden(r, 3, h2a[:, 0], ACT.Gelu)
                    hidden(r, 4, h2a[:, 1], ACT.Gelu)
                    hidden(r, 5, hm[:, 0], ACT.Gelu, vec[:, V_B1:V_B1 + 1])
                    hidden(r, 6, hm[:, 1], ACT.Gelu, vec[:, V_B1 + 1:V_B1 + 2])
                    hidden(r, 7, h3b[:, 0], ACT.Gelu)
                    hidden(r, 8, h3b[:, 1], ACT.Gelu)
                    hidden(r, 9, h2b[:, 0], ACT.Gelu)
                    hidden(r, 10, h2b[:, 1], ACT.Gelu)
                    hidden(r, 11, hm[:, 2], ACT.Gelu, vec[:, V_B1 + 2:V_B1 + 3])
                    hidden(r, 12, hm[:, 3], ACT.Gelu, vec[:, V_B1 + 3:V_B1 + 4])
                    hidden(r, 13, h2c[:, 0], ACT.Gelu)
                    hidden(r, 14, h2c[:, 1], ACT.Gelu)
                if head:
                    evac_maxima(r, 0, R[3])
                    act.wait_ge(conv_dve, at(conv_dve, r, 2 * (TAPS - 1)))
                    act.wait_ge(conv_pool, at(conv_pool, r, 2 * TAPS - 1))
                    act.wait_ge(y_ps, at(y_ps, r, 0))
                    act.wait_ge(c_moved, at(c_moved, r, 0))
                    act.activation(xact[:], cv[:], ACT.Silu).then_inc(conv_sb, 1)
                if tail:
                    act.wait_ge(h1_sb, at(h1_sb, r, 0))
                    act.wait_ge(y_ps, at(y_ps, r, 0))
                    hidden(r, 16, h1a[:, 0], ACT.Silu)
                    hidden(r, 17, h1a[:, 1], ACT.Silu)
                if head:
                    act.wait_ge(z_sb, at(z_sb, r, T))
                    act.wait_ge(spa_sb, at(spa_sb, r, 1))
                    act.activation(zs, zs, ACT.Silu).then_inc(zs_sb, 1)
                    evac_maxima(r, 1, R[1])

            def exponentiate(r, e):
                act.wait_ge(e_ps, at(e_ps, r, e + 1))
                act.wait_ge(pv_ps, at(pv_ps, r, e - 3))
                act.activation(blocks(pr_flat[e % 4], e % UNITS), blocks(S_flat[score_pair(e)], e % UNITS),
                               ACT.Exp).then_inc(p_sb, 1)

            def negative_exp(r):
                act.wait_ge(moe_sb, at(moe_sb, r, T * E))
                act.wait_ge(og_sb, at(og_sb, r, 0))
                act.activation(gs[:], x2[:], ACT.Exp, scale=-1.0).then_inc(gs_sb, 1)

            def square_y(r, c):
                act.wait_ge(yz_sb, at(yz_sb, r, c + 1))
                act.wait_ge(ry_sb, at(ry_sb, r, 1))
                act.wait_ge(yss_sb, at(yss_sb, r, c - 1))
                act.wait_ge(x2ss_sb, at(x2ss_sb, r, 1))
                act.activation(junk[:, c % 2, :], yz[:, c % 2, :], ACT.Square,
                               accum_out=yss[:, c:c + 1]).then_inc(yss_sb, 1)

            def stage_a(r, tail):
                act.preload_act_table_set(EXP_LN)
                act.wait_ge(cum_ps, at(cum_ps, r, 1))
                act.wait_ge(h_sb, at(h_sb, r, 0))
                act.wait_ge(yc_sb, at(yc_sb, r, 0))
                act.wait_ge(xw_sb, at(xw_sb, r, 0))
                act.activation(dec[:].rearrange("p a c h -> p (a c h)"), S[0][:, 0, 0:48],
                               ACT.Exp).then_inc(dec_sb, 1)
                for e in range(G * UNITS):
                    g, u = e // UNITS, e % UNITS
                    exponentiate(r, e)
                    if u == 0 and g > 0:
                        evac_y(r, g - 1)
                    if u == 1 and g > 0:
                        evac_values(r, g - 1)
                    if u == (2 if g == 0 else 1):
                        act.wait_ge(seg_ps, at(seg_ps, r, g + 1))
                        act.wait_ge(wm_sb, at(wm_sb, r, g - 1))
                        act.activation(es[:, g % 2].rearrange("p h t -> p (h t)"), R[1][:, :],
                                       ACT.Exp).then_inc(seg_sb, 1)
                    if u == 1 and g > 0:
                        square_y(r, g - 1)
                    if (g, u) in ((1, 2), (2, 3)):
                        evac_maxima(r, g + 1, R[1])
                    if e == 3 and tail:
                        negative_exp(r)
                    if (g, u) == (3, 3):
                        evac_a(r)
                evac_b(r)
                evac_y(r, T - 1)
                square_y(r, T - 1)
                evac_values(r, G - 1)

            for sem in act_sems:
                act.sem_inc(sem, per[sem.name])
            for sem in (ry_sb, r2_sb, r3_sb, aoT_sb, x2ss_sb, xfT_sb, x1T_sb, gexp_sb, act_up, gs_sb):
                act.sem_inc(sem, per[sem.name])
            act.wait_ge(c_loaded, 48)
            act.wait_ge(pool_set, 3)
            act.preload_act_table_set(EXP_LN)
            act.activation(neg_a[:], row[:, R_ALOG:R_ALOG + NH], ACT.Exp).then_inc(act_set, 1)
            evac_a(-2)
            evac_b(-2)
            stage_b(-1, False, True)
            stage_a(-1, False)
            with act.Fori(0, B - 1) as r:
                stage_b(r, True, True)
                stage_a(r, True)
            stage_b(B - 1, True, False)
            for t in range(T):
                act.wait_ge(moe_sb, at(moe_sb, B - 1, E * (t + 1)))
                act.wait_ge(og_sb, at(og_sb, B - 1, 0))
                act.activation(gs[:, t, :], x2[:, t, :], ACT.Silu).then_inc(last_silu, 1)

        @block.vector
        def _(dve):
            tt, ts, stt = dve.tensor_tensor, dve.tensor_scalar, dve.scalar_tensor_tensor

            def vcol(n):
                return vec[:, n:n + 1]

            def values(r, g, turned, done):
                view = R[3][:, :].rearrange("p (t j x) -> p t j x", t=T, j=4)
                dve.wait_ge(turned, at(turned, r, g + 1 if g < 3 else 1))
                dve.wait_ge(aoT_ps, at(aoT_ps, r, 1 if g < 3 else 0))
                dve.reciprocal(rden[:], view[:, :, :, HD]).then_inc(done, 1)
                dve.wait_ge(done, at(done, r, 2 * g + 1 if g < 3 else 1))
                tt(ao[:, :, 32 * g:32 * g + 32].rearrange("p t (j d) -> p t j d", j=4),
                   view[:, :, :, 0:HD], rden[:].unsqueeze(3).broadcast_to([P, T, 4, HD]),
                   ALU.mult).then_inc(done, 1)

            def maxima(r, m):
                g, u = m // UNITS, m % UNITS
                n, _, heads = UNIT[u]
                dve.wait_ge(s_ps, at(s_ps, r, m + 1))
                dve.tensor_reduce(mx[:, n // P - 1, g, heads[0]:heads[-1] + 1],
                                  blocks(S_flat[m % 2 if g < 2 else 0], u), AX.X, ALU.max,
                                  negate=True).then_inc(mx_sb, 1)

            def split_maxima(r, g):
                dve.wait_ge(mx_sb, at(mx_sb, r, UNITS * (g + 1)))
                dve.wait_ge(mT_ps, at(mT_ps, r, g + 1 - G))
                dve.tensor_copy(mhl[:, g, :, :, 0].bitcast(F32R), mx[:, :, g, :]).then_inc(mhl_sb, 1)
                dve.wait_ge(mhl_sb, at(mhl_sb, r, 2 * g + 1))
                tt(mhl[:, g, :, :, 1], mx[:, :, g, :], mhl[:, g, :, :, 0],
                   ALU.subtract).then_inc(mhl_sb, 1)

            def conv_tap(r, n, k):
                if k == TAPS - 2:
                    dve.wait_ge(conv_act, at(conv_act, r, n + 1))
                else:
                    dve.wait_ge(conv_dve, at(conv_dve, r, (TAPS - 1) * n + 2 - k))
                stt(out=cv[:, n], in0=xc[:, n, k:k + L], scalar=vcol(V_CONVW + TAPS * n + k), in1=cv[:, n],
                    op0=ALU.mult, op1=ALU.add).then_inc(conv_dve, 1)

            def stats(r):
                dve.wait_ge(x_loaded, at(x_loaded, r, 16))
                for t in range(T):
                    i = dve.bn_stats(st6[:, t, :], xin[:, t, :])
                i.then_inc(stat_sb, 1)
                dve.wait_ge(stat_sb, at(stat_sb, r, 1))
                dve.sem_inc(dve_passed, 1)
                for t in range(T):
                    i = dve.bn_aggr(mv[:, t, :], st6[:, t, :])
                i.then_inc(stat_sb, 1)

            def norms(r):
                dve.wait_ge(rn_sb, at(rn_sb, r, 8))
                dve.wait_ge(xaT_ps, at(xaT_ps, r, 0))
                dve.wait_ge(xbT_ps, at(xbT_ps, r, 0))
                for t in range(T):
                    ts(xa[:, t, :], xin[:, t, :], mv[:, t, 0:1], lnv[:, 4, t:t + 1], ALU.subtract, ALU.mult)
                for t in range(T):
                    i = ts(xb[:, t, :], xin[:, t, :], mv[:, t, 0:1], lnv[:, 5, t:t + 1],
                           ALU.subtract, ALU.mult)
                i.then_inc(xab_sb, 1)

            def gate_logits(r):
                flat = [gt[:, n].rearrange("p t e -> p (t e)") for n in range(12)]
                dve.wait_ge(gate_ps, at(gate_ps, r, 1))
                dve.tensor_copy(flat[0], R[2][:, 0:T * E]).then_inc(gate_sb, 1)
                yield
                dve.wait_ge(gate_sb, at(gate_sb, r, 1))
                tt(flat[1], flat[0], flat[0], ALU.is_equal).then_inc(gate_sb, 1)
                yield
                ts(flat[2], flat[0], FMAX, -FMAX, ALU.min, ALU.max).then_inc(gate_sb, 1)
                yield
                dve.wait_ge(gate_sb, at(gate_sb, r, 3))
                tt(flat[3], flat[2], flat[1], ALU.mult).then_inc(gate_sb, 1)
                yield
                dve.wait_ge(gate_sb, at(gate_sb, r, 4))
                dve.tensor_reduce(g1[:, 0, :], gt[:, 3], AX.X, ALU.max).then_inc(gate_sb, 1)
                yield
                dve.wait_ge(gate_sb, at(gate_sb, r, 5))
                tt(gt[:, 4], gt[:, 3], g1[:, 0, :].unsqueeze(2).broadcast_to([P, T, E]),
                   ALU.subtract).then_inc(gate_sb, 1)
                yield

            def gate_weights(r):
                prob = gt[:, 6]
                dve.wait_ge(gexp_sb, at(gexp_sb, r, 1))
                dve.tensor_reduce(g1[:, 1, :], gt[:, 5], AX.X, ALU.add).then_inc(wts_sb, 1)
                yield
                dve.wait_ge(wts_sb, at(wts_sb, r, 1))
                dve.reciprocal(g1[:, 2, :], g1[:, 1, :]).then_inc(wts_sb, 1)
                yield
                dve.wait_ge(wts_sb, at(wts_sb, r, 2))
                tt(prob, gt[:, 5], g1[:, 2, :].unsqueeze(2).broadcast_to([P, T, E]),
                   ALU.mult).then_inc(wts_sb, 1)
                yield
                dve.wait_ge(wts_sb, at(wts_sb, r, 3))
                other = prob.unsqueeze(2).broadcast_to([P, T, E, E])
                own = prob.unsqueeze(3).broadcast_to([P, T, E, E])
                tt(gq[:, 0], other, own, ALU.is_gt).then_inc(wts_sb, 1)
                yield
                tt(gq[:, 1], other, own, ALU.is_equal).then_inc(wts_sb, 1)
                yield
                dve.wait_ge(wts_sb, at(wts_sb, r, 5))
                tt(gq[:, 1], gq[:, 1], before.unsqueeze(1).broadcast_to([P, T, E, E]),
                   ALU.mult).then_inc(wts_sb, 1)
                yield
                dve.wait_ge(wts_sb, at(wts_sb, r, 6))
                tt(gq[:, 0], gq[:, 0], gq[:, 1], ALU.add).then_inc(wts_sb, 1)
                yield
                dve.wait_ge(wts_sb, at(wts_sb, r, 7))
                dve.tensor_reduce(gt[:, 7], gq[:, 0], AX.X, ALU.add).then_inc(wts_sb, 1)
                yield
                dve.wait_ge(wts_sb, at(wts_sb, r, 8))
                stt(out=gt[:, 8], in0=gt[:, 7], scalar=1.5, in1=prob, op0=ALU.is_lt,
                    op1=ALU.mult).then_inc(wts_sb, 1)
                yield
                dve.wait_ge(wts_sb, at(wts_sb, r, 9))
                dve.tensor_reduce(g1[:, 3, :], gt[:, 8], AX.X, ALU.add).then_inc(wts_sb, 1)
                yield
                dve.wait_ge(wts_sb, at(wts_sb, r, 10))
                ts(g1[:, 1, :], g1[:, 3, :], 1e-8, None, ALU.add).then_inc(wts_sb, 1)
                yield
                dve.wait_ge(wts_sb, at(wts_sb, r, 11))
                dve.reciprocal(g1[:, 2, :], g1[:, 1, :]).then_inc(wts_sb, 1)
                yield
                dve.wait_ge(wts_sb, at(wts_sb, r, 12))
                tt(wts[:], gt[:, 8], g1[:, 2, :].unsqueeze(2).broadcast_to([P, T, E]),
                   ALU.mult).then_inc(wts_sb, 1)
                yield

            def time_steps(r):
                dve.wait_ge(spe_sb, at(spe_sb, r, 1))
                ts(sp[:, 3], sp[:, 2], 2.0, None, ALU.add).then_inc(dt_sb, 1)
                yield
                dve.wait_ge(dt_sb, at(dt_sb, r, 1))
                dve.reciprocal(sp[:, 4], sp[:, 3]).then_inc(dt_sb, 1)
                yield
                dve.wait_ge(dt_sb, at(dt_sb, r, 2))
                tt(sp[:, 5], sp[:, 2], sp[:, 4], ALU.mult).then_inc(dt_sb, 1)
                yield
                dve.wait_ge(dt_sb, at(dt_sb, r, 3))
                tt(sp[:, 6], sp[:, 5], sp[:, 5], ALU.mult).then_inc(dt_sb, 1)
                yield
                dve.wait_ge(dt_sb, at(dt_sb, r, 4))
                ts(sp[:, 7], sp[:, 6], 1.0 / 15, None, ALU.mult).then_inc(dt_sb, 1)
                yield
                for n, c in enumerate((13, 11, 9, 7, 5, 3)):
                    dve.wait_ge(dt_sb, at(dt_sb, r, 5 + n))
                    stt(out=sp[:, 7], in0=sp[:, 7], scalar=1.0 / c, in1=sp[:, 6], op0=ALU.add,
                        op1=ALU.mult).then_inc(dt_sb, 1)
                    yield
                dve.wait_ge(dt_sb, at(dt_sb, r, 11))
                stt(out=sp[:, 8], in0=sp[:, 7], scalar=1.0, in1=sp[:, 5], op0=ALU.add,
                    op1=ALU.mult).then_inc(dt_sb, 1)
                yield
                ts(sp[:, 9], sp[:, 0], 0.0, None, ALU.max).then_inc(dt_sb, 1)
                yield
                dve.wait_ge(dt_sb, at(dt_sb, r, 13))
                stt(out=dt[:], in0=sp[:, 8], scalar=2.0, in1=sp[:, 9], op0=ALU.mult,
                    op1=ALU.add).then_inc(dt_sb, 1)
                yield
                dve.wait_ge(dt_sb, at(dt_sb, r, 14))
                dve.wait_ge(cum_ps, at(cum_ps, r, 0))
                dve.wait_ge(rs_sb, at(rs_sb, r, 0))
                tt(dta[:], dt[:], neg_a[:].unsqueeze(1).broadcast_to([P, T, NH]),
                   ALU.mult).then_inc(dt_sb, 1)
                yield

            def stage_b(r, tail, head):
                if tail:
                    values(r, 3, ot3_ps, ao3_sb)
                    dve.wait_ge(op_ps, at(op_ps, r, 1))
                    dve.wait_ge(ry_sb, at(ry_sb, r, 2))
                    dve.wait_ge(xn_sb, at(xn_sb, r, 0))
                    dve.wait_ge(og_sb, at(og_sb, r, 0))
                    for t in range(T):
                        stt(out=x1[:, t, :], in0=R[2][:, t * P:(t + 1) * P], scalar=ry[:, 1, t:t + 1],
                            in1=xn[:, t, :], op0=ALU.mult, op1=ALU.add).then_inc(x1_sb, 1)
                if tail:
                    dve.wait_ge(x1_sb, at(x1_sb, r, T))
                    for t in range(T):
                        i = dve.bn_stats(st2[:, t, :], x1[:, t, :])
                    i.then_inc(ln2_sb, 1)
                    dve.wait_ge(ln2_sb, at(ln2_sb, r, 1))
                    dve.sem_inc(dve_passed, 1)
                    for t in range(T):
                        i = dve.bn_aggr(mv2[:, t, :], st2[:, t, :])
                    i.then_inc(ln2_sb, 1)
                    dve.wait_ge(wo_ps, at(wo_ps, r, 1))
                    tt(x2[:, :, MASKED:D], R[3][:, 0:T * OC].rearrange("p (t c) -> p t c", t=T),
                       xn[:, :, MASKED:D], ALU.add).then_inc(x2_sb, 1)
                    dve.tensor_copy(x2[:, :, 0:MASKED], xn[:, :, 0:MASKED]).then_inc(x2_sb, 1)
                if tail:
                    dve.wait_ge(r2_sb, at(r2_sb, r, 2))
                    dve.wait_ge(x1T_ps, at(x1T_ps, r, 0))
                    for t in range(T):
                        i = ts(x1n[:, t, :], x1[:, t, :], mv2[:, t, 0:1], r2[:, 1, t:t + 1],
                               ALU.subtract, ALU.mult)
                    i.then_inc(x1n_sb, 1)
                if head:
                    dve.wait_ge(sq_sb, at(sq_sb, r, 1))
                    dve.tensor_reduce(rqk[:, 0], sq[:].rearrange("p t a h d -> p (t a h) d"), AX.X,
                                      ALU.add).then_inc(ssqk_sb, 1)
                if tail:
                    dve.wait_ge(r3_sb, at(r3_sb, r, 2))
                    dve.wait_ge(xfT_ps, at(xfT_ps, r, 0))
                    for t in range(T):
                        i = ts(xf[:, t, :], x2[:, t, :], r3[:, 1, t:t + 1], None, ALU.mult)
                    i.then_inc(xf_sb, 1)
                if head:
                    dve.wait_ge(rqk_sb, at(rqk_sb, r, 2))
                    tt(sq[:].rearrange("p t a h d -> p (t a h) d"),
                       qk[:].rearrange("p t a h d -> p (t a h) d"),
                       rqk[:, 2].unsqueeze(2).broadcast_to([P, T * 2 * AH, HD]),
                       ALU.mult).then_inc(nqk_sb, 1)
                    dve.wait_ge(nqk_sb, at(nqk_sb, r, 1))
                    flat = sq[:].rearrange("p t a h d -> p t (a h d)")
                    tt(flat, flat, wqk[:].rearrange("p a h d -> p (a h d)").unsqueeze(1)
                       .broadcast_to([P, T, 2 * D]), ALU.mult).then_inc(nqk_sb, 1)
                    dve.wait_ge(nqk_sb, at(nqk_sb, r, 2))
                    dve.wait_ge(qkT_ps, at(qkT_ps, r, 0))
                gate = gate_logits(r) if tail else iter(())
                next(gate, None)
                for a in range(2):
                    if head:
                        parts = tokqk[:, :, a, :, 0:2 * HD * (1 + a)]
                        dve.tensor_copy(
                            parts.rearrange("p t h (n d) -> p t h n d", d=HD)[:, :, :, ::1 + a].bitcast(F32R),
                            sq[:, :, a].unsqueeze(3).broadcast_to([P, T, AH, 2, HD])).then_inc(nqk_sb, 1)
                    next(gate, None)
                    next(gate, None)
                if head:
                    dve.wait_ge(nqk_sb, at(nqk_sb, r, 4))
                    tt(tokqk[:, :, 0, :, 2 * HD:3 * HD], sq[:, :, 0], tokqk[:, :, 0, :, 0:HD], ALU.subtract)
                next(gate, None)
                if head:
                    tt(tokqk[:, :, 1, :, HD:2 * HD], sq[:, :, 1], tokqk[:, :, 1, :, 0:HD],
                       ALU.subtract).then_inc(lo_sb, 1)
                for _ in gate:
                    pass
                if head:
                    dve.wait_ge(z_sb, at(z_sb, r, T))
                    tt(sp[:, 0], zraw[:, :, DI:DI + NH],
                       row[:, R_DTB:R_DTB + NH].unsqueeze(1).broadcast_to([P, T, NH]),
                       ALU.add).then_inc(spa_sb, 1)
                    dve.wait_ge(spa_sb, at(spa_sb, r, 1))
                    stt(out=sp[:, 1], in0=sp[:, 0], scalar=-1.0, in1=sp[:, 0], op0=ALU.mult,
                        op1=ALU.max).then_inc(spa_sb, 1)
                if head:
                    dve.wait_ge(e_ps, at(e_ps, r, 0))
                    for g in range(G):
                        dve.wait_ge(qkT_ps, at(qkT_ps, r, 2 * g + 2))
                        dve.tensor_copy(kT[:, g, :], bank((2 * g + 1) % 4)).then_inc(kT_sb, 1)
                    dve.wait_ge(xc_sb, at(xc_sb, r, 3))
                    dve.wait_ge(conv_sb, at(conv_sb, r, 0))
                    time = time_steps(r)
                    weights = gate_weights(r) if tail else iter(())
                    for m in range(2 * UNITS):
                        maxima(r, m)
                        if m > 0:
                            next(time, None)
                        if m >= WEIGHTS_FROM:
                            next(weights, None)
                        if m in TAP_AT:
                            conv_tap(r, *TAP_AT[m])
                        if m > 0:
                            next(time, None)
                        if m >= WEIGHTS_FROM:
                            next(weights, None)
                        if m % UNITS == UNITS - 1:
                            split_maxima(r, m // UNITS)
                    for _ in weights:
                        pass
                elif tail:
                    for _ in gate_weights(r):
                        pass
                if tail:
                    for n in range(2):
                        dve.wait_ge(up_ps, at(up_ps, r, 18 + n))
                        dve.wait_ge(act_up, at(act_up, r, 16 + n))
                        dve.wait_ge(moe_ps, at(moe_ps, r, 0))
                        tt(h1[:, n], R[(18 + n) % 4][:, :], h1a[:, n], ALU.mult).then_inc(h1_sb, 1)
                    dve.wait_ge(mlp_ps, at(mlp_ps, r, 1))
                    dve.wait_ge(x1b_sb, at(x1b_sb, r, 1))
                    tt(x1[:], R[0][:, :].rearrange("p (t c) -> p t c", t=T), x1[:],
                       ALU.add).then_inc(sv_sb, 1)
                for t in range(T):
                    if tail:
                        dve.wait_ge(moe_ps, at(moe_ps, r, t + 1))
                        for e in range(E):
                            if e:
                                dve.wait_ge(moe_sb, at(moe_sb, r, E * t + e))
                            else:
                                dve.wait_ge(wts_sb, at(wts_sb, r, 13))
                            stt(out=x2[:, t, MASKED:D], in0=R[(22 + t) % 4][:, e * OC:(e + 1) * OC],
                                scalar=wts[:, t, e:e + 1], in1=x2[:, t, MASKED:D],
                                op0=ALU.mult, op1=ALU.add).then_inc(moe_sb, 1)
                    if head and t < 2:
                        maxima(r, MAX_AT[t])

            def sigmoid(r, step):
                if step == 0:
                    dve.wait_ge(gs_sb, at(gs_sb, r, 1))
                    ts(gs[:], gs[:], 1.0, None, ALU.add).then_inc(gr_sb, 1)
                else:
                    dve.wait_ge(gr_sb, at(gr_sb, r, 1))
                    dve.reciprocal(gs[:, step - 1, :], gs[:, step - 1, :]).then_inc(gr_sb, 1)

            def join(r, step):
                if step == 0:
                    dve.wait_ge(gr_sb, at(gr_sb, r, 1 + T))
                    tt(gs[:], x2[:], gs[:], ALU.mult).then_inc(og_sb, 1)
                elif step == 1:
                    dve.wait_ge(sv_sb, at(sv_sb, r, 1))
                    dve.wait_ge(og_sb, at(og_sb, r, 1))
                    tt(gs[:], x1[:], gs[:], ALU.mult).then_inc(og_sb, 1)
                else:
                    dve.wait_ge(og_sb, at(og_sb, r, 2))
                    dve.wait_ge(xres_loaded, at(xres_loaded, r, 16))
                    tt(xres[:], gs[:], xres[:], ALU.add).then_inc(og_sb, 1)

            def scan_products(r, c):
                dve.wait_ge(xt_ps, at(xt_ps, r, c + 1))
                dve.wait_ge(y_ps, at(y_ps, r, c - 1))
                dve.wait_ge(xw_sb, at(xw_sb, r, c - 1 if c >= 2 else 0))
                dve.wait_ge(hn_ps, at(hn_ps, r, c - 1 if c >= 2 else 0))
                tt(xdt[:, c % 2, :].rearrange("p (h d) -> p h d", h=NH),
                   R[2][:, 0:DI].rearrange("p (h d) -> p h d", h=NH),
                   dt[:, c, :].unsqueeze(2).broadcast_to([P, NH, HP]), ALU.mult).then_inc(xdt_sb, 1)
                dve.tensor_copy(btok[:, c % 2, :], R[2][:, DI:DI + NS])
                tt(gm[:, c % 2, :], R[2][:, 3 * P:4 * P], upto, ALU.mult).then_inc(gm_sb, 1)

            def scan_weights(r, c):
                dve.wait_ge(seg_sb, at(seg_sb, r, c + 1))
                dve.wait_ge(gm_sb, at(gm_sb, r, c + 1))
                dve.wait_ge(y_ps, at(y_ps, r, c - 1))
                tt(wm[:, c % 2], es[:, c % 2], gm[:, c % 2, :].unsqueeze(1).broadcast_to([P, NH, P]),
                   ALU.mult).then_inc(wm_sb, 1)

            def scan_combine(r, c):
                dve.wait_ge(y_ps, at(y_ps, r, c + 1))
                dve.wait_ge(zs_sb, at(zs_sb, r, 1))
                dve.wait_ge(yT_ps, at(yT_ps, r, c - 1))
                dve.wait_ge(yss_sb, at(yss_sb, r, c - 1))
                if c == 0:
                    y = R[3][:, 0:DI]
                else:
                    tt(yc[:, 0, :].rearrange("p (h d) -> p h d", h=NH),
                       R[3][:, DI:2 * DI].rearrange("p (h d) -> p h d", h=NH),
                       dec[:, 0, c, :].unsqueeze(2).broadcast_to([P, NH, HP]), ALU.mult)\
                        .then_inc(yc_sb, 1)
                    dve.wait_ge(yc_sb, at(yc_sb, r, 2 * c - 1))
                    tt(yc[:, 1, :], R[3][:, 0:DI], yc[:, 0, :], ALU.add).then_inc(yc_sb, 1)
                    dve.wait_ge(yc_sb, at(yc_sb, r, 2 * c))
                    y = yc[:, 1, :]
                tt(yz[:, c % 2, :], y, zraw[:, c, 0:DI], ALU.mult).then_inc(yz_sb, 1)

            def scan_state(r, c):
                dve.wait_ge(hn_ps, at(hn_ps, r, c + 1))
                if c == 0:
                    dve.tensor_copy(hst[:], R[1][0:NS, 0:DI]).then_inc(h_sb, 1)
                else:
                    tt(hdec[:].rearrange("p (h d) -> p h d", h=NH),
                       hst[:].rearrange("p (h d) -> p h d", h=NH),
                       dec[0:NS, 2, c, :].unsqueeze(2).broadcast_to([NS, NH, HP]),
                       ALU.mult).then_inc(h_sb, 1)
                    dve.wait_ge(h_sb, at(h_sb, r, 2 * c))
                    tt(hst[:], R[1][0:NS, 0:DI], hdec[:], ALU.add).then_inc(h_sb, 1)

            def stage_a(r, tail):
                dve.wait_ge(rn_sb, at(rn_sb, r, 0))
                for t in range(T):
                    i = ts(xn[:, t, :], xin[:, t, :], mv[:, t, 0:1], lnv[:, 1, t:t + 1],
                           ALU.subtract, ALU.mult)
                i.then_inc(xn_sb, 1)
                for e in range(G * UNITS):
                    g, u = e // UNITS, e % UNITS
                    if u == 5:
                        scan_combine(r, g)
                    if e in MAX_AT and e > 1:
                        maxima(r, MAX_AT[e])
                        if MAX_AT[e] % UNITS == UNITS - 1:
                            split_maxima(r, MAX_AT[e] // UNITS)
                    if u == 1:
                        scan_products(r, g)
                    if u == 2:
                        scan_weights(r, g)
                    if u == 3 and g >= 1:
                        values(r, g - 1, ot_ps, ao_sb)
                    if u == 5 and g < T - 1:
                        scan_state(r, g)
                    if e in SIGMOID_AT and tail:
                        sigmoid(r, SIGMOID_AT.index(e))
                    if e in JOIN_AT and tail:
                        join(r, JOIN_AT.index(e))
                    if e == STATS_AT:
                        stats(r)
                    if e == NORM_AT[-1] + 2:
                        norms(r)

            for sem in dve_sems:
                dve.sem_inc(sem, per[sem.name])
            for sem in (ao3_sb, x1_sb, ln2_sb, x2_sb, xf_sb, x1n_sb, gate_sb, wts_sb, h1_sb, sv_sb, moe_sb, gr_sb, og_sb):
                dve.sem_inc(sem, per[sem.name])
            stats(-2)
            dve.wait_ge(c_loaded, 48)
            dve.tensor_copy(identb[:], ident).then_inc(dve_set, 1)
            dve.tensor_copy(maskb[:], future).then_inc(dve_set, 1)
            for n, (col, scale) in enumerate(((R_QN, HD ** -0.5), (R_KN, 1.0))):
                ts(wqk[:, n], row[:, col:col + HD].unsqueeze(1).broadcast_to([P, AH, HD]), scale, None,
                   ALU.mult).then_inc(dve_set, 1)
            for n in range(2):
                ts(diag_d[:, n, :], ident, vcol(V_DCH + n), None, ALU.mult).then_inc(dve_set, 1)
            dve.wait_ge(act_set, 1)
            ts(neg_a[:], neg_a[:], -1.0, None, ALU.mult).then_inc(dve_set, 1)
            norms(-2)
            dve.wait_ge(dve_set, 7)
            stage_b(-1, False, True)
            stage_a(-1, False)
            with dve.Fori(0, B - 1) as r:
                stage_b(r, True, True)
                stage_a(r, True)
            stage_b(B - 1, True, False)
            dve.wait_ge(sv_sb, at(sv_sb, B - 1, 1))
            dve.wait_ge(xres_loaded, at(xres_loaded, B - 1, 16))
            for t in range(T):
                dve.wait_ge(last_silu, t + 1)
                tt(gs[:, t, :], x1[:, t, :], gs[:, t, :], ALU.mult).then_inc(last_join, 1)
                dve.wait_ge(last_join, 2 * t + 1)
                tt(xres[:, t, :], gs[:, t, :], xres[:, t, :], ALU.add).then_inc(last_join, 1)

        @block.gpsimd
        def _(pool):
            tt, ts = pool.tensor_tensor, pool.tensor_scalar

            def first_norms(r, step):
                var = mv[:, :, 1]
                if step == 0:
                    pool.wait_ge(stat_sb, at(stat_sb, r, 2))
                    pool.wait_ge(xn_sb, at(xn_sb, r, 1))
                    pool.wait_ge(xab_sb, at(xab_sb, r, 0))
                    pool.sem_inc(pool_passed, 1)
                    ts(lnv[:, 0, :], var, 1.0, EPS, ALU.mult, ALU.add).then_inc(rn_sb, 1)
                    pool.wait_ge(rn_sb, at(rn_sb, r, 1))
                    tt(lnv[:, 1, :], lnv[:, 0, :], minus_half[:, 0:T], ALU.pow).then_inc(rn_sb, 1)
                elif step == 1:
                    pool.wait_ge(rn_sb, at(rn_sb, r, 2))
                    tt(lnv[:, 2, :], lnv[:, 1, :], lnv[:, 1, :], ALU.mult).then_inc(rn_sb, 1)
                    pool.wait_ge(rn_sb, at(rn_sb, r, 3))
                    tt(lnv[:, 3, :], lnv[:, 2, :], var, ALU.mult).then_inc(rn_sb, 1)
                    pool.wait_ge(rn_sb, at(rn_sb, r, 4))
                    pool.sem_inc(pool_passed, 1)
                    ts(lnv[:, 4, :], lnv[:, 3, :], 1.0, EPS, ALU.mult, ALU.add).then_inc(rn_sb, 1)
                    ts(lnv[:, 5, :], lnv[:, 3, :], 1.0, EPS_RMS, ALU.mult, ALU.add).then_inc(rn_sb, 1)
                else:
                    pool.wait_ge(rn_sb, at(rn_sb, r, 6))
                    tt(lnv[:, 6:8, :].rearrange("p a t -> p (a t)"),
                       lnv[:, 4:6, :].rearrange("p a t -> p (a t)"), minus_half[:],
                       ALU.pow).then_inc(rn_sb, 1)
                    pool.wait_ge(rn_sb, at(rn_sb, r, 7))
                    tt(lnv[:, 4:6, :], lnv[:, 6:8, :], lnv[:, 1, :].unsqueeze(1).broadcast_to([P, 2, T]),
                       ALU.mult).then_inc(rn_sb, 1)

            def stage_b(r, tail, head):
                if tail:
                    pool.wait_ge(x1n_sb, at(x1n_sb, r, 1))
                    tt(x1[:], x1[:], row[:, R_B2:R_B2 + D].unsqueeze(1).broadcast_to([P, T, D]),
                       ALU.add).then_inc(x1b_sb, 1)
                if head:
                    pool.wait_ge(xc_sb, at(xc_sb, r, 3))
                    pool.wait_ge(conv_sb, at(conv_sb, r, 0))
                    pool.sem_inc(pool_passed, 1)
                    n = 2
                    ts(cv[:, n], xc[:, n, 3:3 + L], vec[:, V_CONVW + 4 * n + 3:V_CONVW + 4 * n + 4],
                       vec[:, V_CONVB + n:V_CONVB + n + 1], ALU.mult, ALU.add).then_inc(conv_pool, 1)
                    for i, k in enumerate((2, 1, 0)):
                        tap = V_CONVW + 4 * n + k
                        if i:
                            pool.wait_ge(conv_pool, at(conv_pool, r, 2 * i + 1))
                            pool.sem_inc(pool_passed, 1)
                        ts(cm[:], xc[:, n, k:k + L], vec[:, tap:tap + 1], 0.0, ALU.mult,
                           ALU.add).then_inc(conv_pool, 1)
                        pool.wait_ge(conv_pool, at(conv_pool, r, 2 * i + 2))
                        tt(cv[:, n], cv[:, n], cm[:], ALU.add).then_inc(conv_pool, 1)

            def decays(r, c, tail):
                pool.wait_ge(dt_sb, at(dt_sb, r, 15))
                if c == 0 and tail:
                    pool.wait_ge(up_ps, at(up_ps, r, 11))
                pool.wait_ge(seg_ps, at(seg_ps, r, c - 1))
                tt(rs[:, c % 2], upto.unsqueeze(1).broadcast_to([P, NH, P]),
                   dta[:, c, :].unsqueeze(2).broadcast_to([P, NH, P]), ALU.mult).then_inc(rs_sb, 1)

            def stage_a(r, tail):
                decays(r, 0, tail)
                for e in range(G * UNITS):
                    g, u = e // UNITS, e % UNITS
                    pool.wait_ge(p_sb, at(p_sb, r, e + 1))
                    pool.sem_inc(pool_passed, 1)
                    keep = blocks(pr_flat[e % 4], u, P)
                    pool.affine_select(out=keep, in_=keep, compare_op=ALU.is_ge, fill=0.0, base=0,
                                       pattern=[[0, len(UNIT[u][2])], [1, P]], channel_multiplier=-1)\
                        .then_inc(pm_sb, 1)
                    if u == 2 and g < T - 1:
                        pool.wait_ge(xdt_sb, at(xdt_sb, r, g + 1))
                        pool.wait_ge(dec_sb, at(dec_sb, r, 1))
                        pool.wait_ge(hn_ps, at(hn_ps, r, g - 1 if g >= 2 else 0))
                        tt(xw[:, g % 2, :].rearrange("p (h d) -> p h d", h=NH),
                           xdt[:, g % 2, :].rearrange("p (h d) -> p h d", h=NH),
                           dec[:, 1, g, :].unsqueeze(2).broadcast_to([P, NH, HP]),
                           ALU.mult).then_inc(xw_sb, 1)
                    if u == 3 and g < T - 1:
                        decays(r, g + 1, tail)
                    if e in NORM_AT:
                        first_norms(r, NORM_AT.index(e))

            for sem in pool_sems:
                pool.sem_inc(sem, per[sem.name])
            for sem in (x1b_sb,):
                pool.sem_inc(sem, per[sem.name])
            pool.memset(minus_half[:], -0.5).then_inc(pool_set, 1)
            pool.memset(eps[:, 0:1], EPS).then_inc(pool_set, 1)
            pool.memset(eps[:, 1:2], EPS_RMS).then_inc(pool_set, 1)
            for step in range(3):
                first_norms(-2, step)
            pool.memset(va[:], 0.0).then_inc(pool_set, 1)
            pool.memset(tokqk[:], 0.0).then_inc(pool_set, 1)
            pool.memset(xc[:, :, 0:3], 0.0).then_inc(pool_set, 1)
            pool.wait_ge(pool_set, 5)
            pool.memset(va[:, :, :, HD:HD + 1], 1.0).then_inc(pool_set, 1)
            pool.memset(tokqk[:, :, 1, :, 3 * HD:3 * HD + 2], 1.0).then_inc(pool_set, 1)
            pool.wait_ge(c_loaded, 48)
            stage_b(-1, False, True)
            stage_a(-1, False)
            with pool.Fori(0, B - 1) as r:
                stage_b(r, True, True)
                stage_a(r, True)
            stage_b(B - 1, True, False)


def kernel(**inputs):
    import numpy as np
    import concourse.bacc as bacc
    from concourse.bass_utils import run_bass_kernel_spmd

    a = {k.removeprefix("L0_"): np.asarray(v) for k, v in inputs.items()}
    f32 = np.float32

    def halves(m, n):
        return np.concatenate([m[i * P:(i + 1) * P] for i in range(n)], axis=1)

    proj = a["attn_in_proj_w"].T
    blocks = {
        "qkv": np.concatenate([a["ffn_wq"].T, a["ffn_wk"].T, a["ffn_wv"].T], axis=1),
        "x": proj[:, DI:DI + CONV],
        "zdt": np.concatenate([proj[:, 0:DI], proj[:, DI + CONV:]], axis=1),
        "wo": a["ffn_wo"].T[:, MASKED:],
        "op": halves(a["attn_out_proj_w"].T, 2),
        "gate": a["ffn_gate_w"].T,
        "e0u": a["ffn_e0_up"].T,
        "e3a": a["ffn_e3_down"].T,
        "e2a": a["ffn_e2_l1"].T,
        "w1": a["attn_mlp_w1"].T,
        "e3b": a["ffn_e3_up"].T,
        "e2b": halves(a["ffn_e2_l2"].T, 2),
        "e2c": halves(a["ffn_e2_l3"].T, 2),
        "e1a": a["ffn_e1_w1"].T,
        "e1b": a["ffn_e1_w2"].T,
        "w2": halves(a["attn_mlp_w2"].T, 4),
        "e0d": halves(a["ffn_e0_down"].T[:, MASKED:], 2),
        "e1d": halves(a["ffn_e1_down"].T[:, MASKED:], 2),
        "e2d": halves(a["ffn_e2_l4"].T[:, MASKED:], 2),
        "e3d": halves(a["ffn_e3_out"].T[:, MASKED:], 2),
    }
    weights = np.ascontiguousarray(np.concatenate([blocks[n] for n in W_COLS], axis=1))

    def cols(v, n=1):
        return v.reshape(n, P).T

    vectors = np.ascontiguousarray(np.concatenate([
        cols(a["attn_ln1_w"]), cols(a["attn_ln1_b"]), cols(a["ffn_n1_w"]), cols(a["attn_ln2_w"]),
        cols(a["attn_ln2_b"]), cols(a["ffn_n2_w"]), cols(a["attn_mlp_b1"], 4), cols(a["attn_norm_w"], 2),
        cols(a["attn_conv_b"], 3), halves(a["attn_conv_w"], 3), cols(np.repeat(a["attn_D"], HP), 2)], axis=1))
    rows = np.ascontiguousarray(np.broadcast_to(np.concatenate([
        a["attn_dt_bias"], a["attn_A_log"], a["ffn_qn_w"], a["ffn_kn_w"], a["attn_mlp_b2"]]), (P, R_TOTAL)))
    at = np.arange(P)
    consts = np.concatenate([
        np.eye(P), at[:, None] <= at, at[:, None] > at, np.ones((P, P)), np.where(at > at[:, None], NEG, 0.0),
        np.broadcast_to((np.arange(E) < np.arange(E)[:, None]).reshape(1, E * E), (P, E * E))],
        axis=1).astype(f32)

    nc = bacc.Bacc("TRN2", target_bir_lowering=False, num_devices=1)
    arrays = {"x": np.ascontiguousarray(a["attn_x"]), "weights": weights, "vectors": vectors, "rows": rows,
              "consts": consts}
    aps = [nc.dram_tensor(n, v.shape, mybir.dt.from_np(v.dtype), kind="ExternalInput").ap()
           for n, v in arrays.items()]
    out = nc.dram_tensor("out", (B, L, D), F32, kind="ExternalOutput").ap()
    build(nc, *aps, out)
    r = run_bass_kernel_spmd(nc, [arrays], core_ids=[0])
    return r.results[0]["out"]
```
